# Optimizing a Trainium2 kernel written in Bass

```python
import numpy as np
import jax
import jax.numpy as jnp

def _softmax(x, axis=-1):
    return jax.nn.softmax(x, axis=axis)

def _gelu(x):
    return jax.nn.gelu(x, approximate=True)

def _silu(x):
    return jax.nn.silu(x)

def _sigmoid(x):
    return jax.nn.sigmoid(x)

def _layernorm(x, axis=-1, eps=1e-05):
    m = jnp.mean(x, axis=axis, keepdims=True)
    v = jnp.var(x, axis=axis, keepdims=True)
    return (x - m) / jnp.sqrt(v + eps)

def _scatter_add(tgt, idx, src, axis=0):
    return tgt.at[idx].add(src)

def _segment_sum(src, seg, n):
    return jax.ops.segment_sum(src, seg, n)
kernel_name = 'mk_sandwich_d1_jaxref_r8_a56e11'

def setup_inputs(seed: int=0):
    np.random.seed(seed)
    _w = jnp.asarray

    def _L0_attn_setup():
        import jax, jax.numpy as jnp
        import numpy as np
        DIM = 128
        BATCH = 4
        SEQ = 512
        key = jax.random.key(seed)
        ks = jax.random.split(key, 5)
        s = 1.0 / np.sqrt(DIM)
        x = jax.random.normal(ks[0], (BATCH, SEQ, DIM), dtype=jnp.float32)
        W_in = jax.random.uniform(ks[1], (DIM, DIM), jnp.float32, -s, s)
        b_in = jax.random.uniform(ks[2], (DIM,), jnp.float32, -s, s)
        W_out = jax.random.uniform(ks[3], (DIM, DIM), jnp.float32, -s, s)
        b_out = jax.random.uniform(ks[4], (DIM,), jnp.float32, -s, s)
        decay = jnp.float32(0.25)
        mix = jnp.float32(0.5)
        return {'x': x, 'W_in': W_in, 'b_in': b_in, 'W_out': W_out, 'b_out': b_out, 'decay': decay, 'mix': mix}
    _L0_attn_in = _L0_attn_setup()

    def _L0_ffn_setup():
        import jax, jax.numpy as jnp
        import numpy as np
        E = 8
        TOPK = 2
        D = 128
        F = 512
        B, S = (2, 64)

        def _gmm(x, W, expert_onehot):
            return jnp.einsum('te,td,edf->tf', expert_onehot, x, W)
        key = jax.random.key(seed)
        k1, k2, k3, k4, k5 = jax.random.split(key, 5)
        scale_d = 1.0 / np.sqrt(D)
        scale_f = 1.0 / np.sqrt(F)
        return {'inputs': jax.random.normal(k1, (B, S, D), jnp.float32), 'gate_kernel': jax.random.normal(k2, (D, E), jnp.float32) * scale_d, 'w0': jax.random.normal(k3, (E, D, F), jnp.float32) * scale_d, 'w1': jax.random.normal(k4, (E, D, F), jnp.float32) * scale_d, 'wo': jax.random.normal(k5, (E, F, D), jnp.float32) * scale_f}
    _L0_ffn_in = _L0_ffn_setup()
    _d = {'L0_attn_x': _L0_attn_in['x'], 'L0_attn_W_in': _L0_attn_in['W_in'], 'L0_attn_b_in': _L0_attn_in['b_in'], 'L0_attn_W_out': _L0_attn_in['W_out'], 'L0_attn_b_out': _L0_attn_in['b_out'], 'L0_attn_decay': _L0_attn_in['decay'], 'L0_attn_mix': _L0_attn_in['mix'], 'L0_ffn_gate_kernel': _L0_ffn_in['gate_kernel'], 'L0_ffn_w0': _L0_ffn_in['w0'], 'L0_ffn_w1': _L0_ffn_in['w1'], 'L0_ffn_wo': _L0_ffn_in['wo']}
    _x0 = _d['L0_attn_x']
    _d['L0_attn_x'] = jax.random.normal(jax.random.fold_in(jax.random.key(seed), 1), (8, 512, 128), dtype=_x0.dtype)
    del _x0
    return _d

def reference(L0_attn_x, L0_attn_W_in, L0_attn_b_in, L0_attn_W_out, L0_attn_b_out, L0_attn_decay, L0_attn_mix, L0_ffn_gate_kernel, L0_ffn_w0, L0_ffn_w1, L0_ffn_wo):

    def _L0_attn_ref(x, W_in, b_in, W_out, b_out, decay, mix):
        import jax, jax.numpy as jnp
        import numpy as np
        DIM = 128
        BATCH = 4
        SEQ = 512
        shifted = jnp.pad(x, ((0, 0), (1, 0), (0, 0)))[:, :-1]
        inp = mix * x + (1.0 - mix) * shifted
        h = jax.nn.relu(jnp.einsum('bsd,ed->bse', inp, W_in) + b_in)

        def step(state, h_t):
            state = state * decay + h_t
            return (state, state)
        h_t_major = jnp.swapaxes(h, 0, 1)
        _, states = jax.lax.scan(step, jnp.zeros((x.shape[0], x.shape[2]), x.dtype), h_t_major)
        states = jnp.swapaxes(states, 0, 1)
        return jnp.einsum('bsd,ed->bse', states, W_out) + b_out

    def _L0_ffn_ref(inputs, gate_kernel, w0, w1, wo):
        import jax, jax.numpy as jnp
        import numpy as np
        E = 8
        TOPK = 2
        D = 128
        F = 512
        B, S = (2, 64)

        def _gmm(x, W, expert_onehot):
            return jnp.einsum('te,td,edf->tf', expert_onehot, x, W)
        dtype = inputs.dtype
        gate_logits = jnp.einsum('bsd,de->bse', inputs, gate_kernel)
        weights, selected_experts = jax.lax.top_k(gate_logits, TOPK)
        weights = jax.nn.softmax(weights.astype(jnp.float32), axis=-1).astype(dtype)
        inputs_2d = jnp.reshape(inputs, (-1, D))
        flat_sel = jnp.ravel(selected_experts)
        sort_idx = jnp.argsort(flat_sel)
        rep = jnp.repeat(inputs_2d, TOPK, axis=0)
        sorted_hidden = jnp.take(rep, sort_idx, axis=0)
        T = flat_sel.shape[0]
        group_sizes = jnp.zeros((E,), jnp.int32).at[flat_sel].add(1)
        expert_ids = jnp.repeat(jnp.arange(E), group_sizes, total_repeat_length=T)
        onehot = jax.nn.one_hot(expert_ids, E, dtype=dtype)
        layer_1 = _gmm(sorted_hidden, w0, onehot)
        layer_2 = _gmm(sorted_hidden, w1, onehot)
        intermediate = jax.nn.silu(layer_1) * layer_2
        layer_3 = _gmm(intermediate, wo, onehot)
        unsort = jnp.take(layer_3, jnp.argsort(sort_idx), axis=0)
        combined = unsort * jnp.ravel(weights)[:, None]
        out = jnp.sum(combined.reshape(-1, TOPK, D), axis=1)
        return out.reshape(inputs.shape).astype(dtype)
    x = L0_attn_x
    x = x + _layernorm(_L0_attn_ref(_layernorm(x, axis=-1), L0_attn_W_in, L0_attn_b_in, L0_attn_W_out, L0_attn_b_out, L0_attn_decay, L0_attn_mix), axis=-1)
    x = x + _layernorm(_L0_ffn_ref(_layernorm(x, axis=-1), L0_ffn_gate_kernel, L0_ffn_w0, L0_ffn_w1, L0_ffn_wo), axis=-1)
    return x

_drawn_inputs = setup_inputs


def setup_inputs(seed=0):
    import zlib

    import numpy as np

    out = dict(_drawn_inputs(seed))
    spreads = {}
    factors = {}
    for name, (base, spread) in spreads.items():
        noise = np.random.default_rng([zlib.crc32(name.encode()), seed]).standard_normal(out[name].shape)
        drawn = base * np.exp(spread * noise) if base else spread * noise
        out[name] = jnp.asarray(drawn.astype(out[name].dtype))
    for name, factor in factors.items():
        out[name] = (out[name] * factor).astype(out[name].dtype)
    return out
```

```python
from contextlib import ExitStack

import concourse.bass as bass
from concourse import mybir

F32 = mybir.dt.float32
BF16 = mybir.dt.bfloat16
I32 = mybir.dt.int32
U32 = mybir.dt.uint32
ALU = mybir.AluOpType
ACT = mybir.ActivationFunctionType
AX = mybir.AxisListType

P = 128
B, S, D = 8, 512, 128
E, F, K = 8, 512, 2
T = B * S
G = S // P
FC = F // P
EPS = 1e-5
REGION = T + P
ROW = D + 2
UNROLL = 8
TILES = -(-(T * K // P + E - 1) // UNROLL) * UNROLL
SPARE = TILES - T * K // P
NO_PAIR = 2 * K * T
Y_SLOTS = 4


def sandwich_kernel(nc, x_in, w_in_in, b_in_in, w_out_in, b_out_in, decay_in, mix_in,
                    gate_in, w0_in, w1_in, wo_in, out):
    ctx = ExitStack()
    with ctx:
        def sb(name, shape, dt=F32):
            return ctx.enter_context(nc.sbuf_tensor("sb_" + name, shape, dt))

        def sem(name):
            return ctx.enter_context(nc.semaphore(name))

        def pair(name, shape, dt=F32):
            return [sb(f"{name}{n}", shape, dt) for n in range(2)]

        expert_rows = nc.dram_tensor("expert_rows", [E * REGION + SPARE * P, ROW], F32)
        pair_rows = nc.dram_tensor("pair_rows", [T * K, D], F32)

        x = sb("x", [P, B * G, D])
        w0 = sb("w0", [P, E * F])
        w1 = sb("w1", [P, E * F])
        wo = sb("wo", [P, E * FC * D])
        w_in = sb("w_in", [P, D])
        w_out = sb("w_out", [P, D])
        w_inT = sb("w_inT", [P, D])
        w_outT = sb("w_outT", [P, D])
        gate = sb("gate", [P, E])
        b_in = sb("b_in", [P, 1])
        b_out4 = sb("b_out4", [1, G, D])
        decay = sb("decay", [P, 1])
        mix = sb("mix", [P, 1])
        one_minus_mix = sb("one_minus_mix", [P, 1])
        decay_row = sb("decay_row", [P, S])
        ident = sb("ident", [P, P])
        ones_f = sb("ones_f", [P, P])
        ones_b = sb("ones_b", [P, P], BF16)
        before_b = sb("before_b", [P, P], BF16)
        eps = sb("eps", [P, 1])
        expert_i = sb("expert_i", [P, E], I32)
        expert_f = sb("expert_f", [P, E])
        region_f = sb("region_f", [P, E])
        token2_i = sb("token2_i", [P, B * G], I32)
        token2_f = sb("token2_f", [P, B * G])
        tile_i = sb("tile_i", [P, TILES], I32)
        tile_f = sb("tile_f", [P, TILES])
        pad_row = sb("pad_row", [P, ROW])

        stats1, stats2, stats3 = (pair(f"stats{n}_", [P, G, 6]) for n in (1, 2, 3))
        mv1, mv2, mv3 = (pair(f"mv{n}_", [P, G, 2]) for n in (1, 2, 3))
        sd1, sd2, sd3 = (pair(f"sd{n}_", [P, G]) for n in (1, 2, 3))
        rs1, rs2, rs3 = (pair(f"rs{n}_", [P, G]) for n in (1, 2, 3))
        nm2 = pair("nm2_", [P, G])
        xn1 = pair("xn1_", [P, G, D])
        shifted = pair("shifted", [P, S])
        mixed = pair("mixed", [P, S])
        hidden = pair("hidden", [P, S])
        states = pair("states", [P, S])
        normed2 = pair("normed2_", [P, G, D])
        row = pair("row", [P, G, ROW])
        xn2T = pair("xn2T", [P, S])
        top8 = pair("top8_", [P, G, 8])
        choice8 = pair("choice8_", [P, G, 8], U32)
        choice_f = pair("choice_f", [P, K, G])
        onehot = pair("onehot", [P, K, G, E], BF16)
        taken = pair("taken", [P, G + 1, E], BF16)
        rank_f = pair("rank_f", [P, G, E])
        place4 = pair("place4_", [P, K, G, E])
        place = pair("place", [P, K, G], I32)
        logit_gap = sb("logit_gap", [P, B * G])
        weight = sb("weight", [P, K, B * G])
        denom = sb("denom", [P, B * G])

        count = sb("count", [P, E])
        count_i = sb("count_i", [P, E], I32)
        tiles_i = sb("tiles_i", [P, E], I32)
        tiles_f = sb("tiles_f", [P, E])
        ends = sb("ends", [P, E])
        skip = sb("skip", [P, E])
        past = sb("past", [P, TILES, E])
        past_skip = sb("past_skip", [P, TILES, E])
        tile_expert = sb("tile_expert", [P, TILES])
        tile_column = sb("tile_column", [P, TILES])
        tile_column_i = sb("tile_column_i", [P, TILES], I32)
        tile_row = sb("tile_row", [P, TILES])
        tile_row_i = sb("tile_row_i", [P, TILES], I32)
        pad_start = sb("pad_start", [P, E])
        pad_start_i = sb("pad_start_i", [P, E], I32)

        taken_rows = [sb(f"taken_rows{n}", [P, ROW]) for n in range(UNROLL)]
        xeT = pair("xeT", [P, P])
        silu = pair("silu", [P, F])
        gated = pair("gated", [P, F])
        gatedT = pair("gatedT", [P, F])
        y_rows = [sb(f"y_rows{n}", [P, D]) for n in range(Y_SLOTS)]
        y_pair = [sb(f"y_pair{n}", [P, 1], I32) for n in range(Y_SLOTS)]

        pairs_in = pair("pairs_in", [P, G, K, D])
        first_part = pair("first_part", [P, G, D])
        moe = pair("moe", [P, G, D])
        normed4 = pair("normed4_", [P, G, D])
        stats4, mv4 = pair("stats4_", [P, G, 6]), pair("mv4_", [P, G, 2])
        sd4, rs4, nm4 = pair("sd4_", [P, G]), pair("rs4_", [P, G]), pair("nm4_", [P, G])

        bank = [ctx.enter_context(nc.psum_tensor(f"bank{n}", [P, 512], F32)) for n in range(8)]
        p_xn1T, p_hidden, p_attn, p_xn2T, p_gate, p_rank = bank[:6]
        p_xeT, p_l1, p_l2, p_gatedT, p_y = bank[:5]

        s_x0, s_x1, s_x2 = sem("x_batch0_in"), sem("x_batch1_in"), sem("x_rest_in")
        s_small, s_experts_in = sem("small_in"), sem("experts_in")
        s_pool_const, s_pool_step, s_const = sem("pool_const"), sem("pool_step"), sem("const")
        s_wT_ps, s_wT = sem("wT_ps"), sem("wT")
        s_apart = sem("waited_apart")
        names_a = ("stats1 mv1 sd1 rs1 xn1 xn1T_ps shifted mixed hidden_ps hidden states attn_ps "
                   "stats2 mv2 sd2 rs2 nm2 normed2 x1 stats3 mv3 sd3 rs3 xn2 xn2T_ps xn2T gate_ps "
                   "top8 choice onehot taken total rank_ps rank place4 place row_done")
        a = {n: sem("a_" + n) for n in names_a.split()}
        s_sent = [sem("rows_sent_even"), sem("rows_sent_odd")]
        s_count_ps, s_b, s_table, s_pads = sem("count_ps"), sem("b_step"), sem("table"), sem("pads")
        s_exp, s_weights = sem("exp"), sem("weights")
        names_c = "xeT_ps xeT l1_ps l2_ps silu gated gatedT_ps gatedT y_ps y"
        c = {n: sem("c_" + n) for n in names_c.split()}
        s_rows_in = [sem(f"tile_in{n}") for n in range(UNROLL)]
        s_y_sent = [sem(f"y_sent{n}") for n in range(Y_SLOTS)]
        names_d = "first moe stats mv sd rs nm normed out"
        d = {n: sem("d_" + n) for n in names_d.split()}
        s_pairs_in = [sem("pairs_in_even"), sem("pairs_in_odd")]
        s_out = sem("out_written")

        def wait(eng, s, value):
            if not (isinstance(value, int) and value <= 0):
                eng.wait_ge(s, value)

        def wait_apart(eng, s, value):
            eng.wait_ge(s, value).then_inc(s_apart, 1)

        def in_range(n, count):
            return not isinstance(n, int) or 0 <= n < count

        def rounds_of_batches(eng, a_round):
            for i in (0, 1):
                a_round(i, i)
            with eng.Fori(2, B - 1, 2) as i:
                for r in (0, 1):
                    a_round(i + r, r)
            for i in (B, B + 1):
                a_round(i, i % 2)

        def rounds_of_tiles(eng, a_round):
            for k in range(UNROLL):
                a_round(0, k)
            with eng.Fori(UNROLL, TILES - UNROLL + 1, UNROLL) as base:
                for r in range(UNROLL):
                    a_round(base, r)
            for k in range(3):
                a_round(TILES, k)

        def tiles_of(t, b):
            return t[:, bass.ds(b * G, G)]

        block = ctx.enter_context(nc.Block())

        @block.sync
        def _(sp):
            tokens = x_in.rearrange("b (j p) d -> p (b j) d", p=P)
            sp.dma_start(x[:, 0:G], tokens[:, 0:G]).then_inc(s_x0, 16)
            sp.dma_start(x[:, G:2 * G], tokens[:, G:2 * G]).then_inc(s_x1, 16)
            sp.dma_start(x[:, 2 * G:], tokens[:, 2 * G:]).then_inc(s_x2, 16)
            sp.dma_start(w0[:].rearrange("p (e f) -> p e f", e=E),
                         w0_in.rearrange("e d f -> d e f")).then_inc(s_experts_in, 16)
            sp.dma_start(w1[:].rearrange("p (e f) -> p e f", e=E),
                         w1_in.rearrange("e d f -> d e f")).then_inc(s_experts_in, 16)
            sp.dma_start(wo[:].rearrange("p (e c n) -> p e c n", e=E, c=FC),
                         wo_in.rearrange("e (c p) n -> p e c n", p=P)).then_inc(s_experts_in, 16)

            sp.wait_ge(s_b, 2)
            for e in range(E):
                first = sp.value_load(pad_start_i[0:1, e:e + 1], min_val=e * REGION,
                                      max_val=e * REGION + T)
                sp.dma_start(expert_rows[bass.ds(first, P), :], pad_row[:]).then_inc(s_pads, 16)
            sp.wait_ge(s_sent[0], 16 * K * G * (B // 2))
            sp.wait_ge(s_sent[1], 16 * K * G * (B // 2) + 16 * SPARE)
            sp.wait_ge(s_pads, 16 * E)
            sp.wait_ge(s_table, 1)

            def load_tile(t, r):
                first = sp.value_load(tile_row_i[0:1, bass.ds(t, 1)], min_val=0,
                                      max_val=E * REGION + (SPARE - 1) * P)
                sp.dma_start(taken_rows[r][:],
                             expert_rows[bass.ds(first, P), :]).then_inc(s_rows_in[r], 16)

            for r in range(UNROLL):
                load_tile(r, r)
            with sp.Fori(UNROLL, TILES - UNROLL + 1, UNROLL) as base:
                for r in range(UNROLL):
                    sp.wait_ge(c["y"], base + (r - UNROLL + 1))
                    load_tile(base + r, r)

            for n in range(Y_SLOTS):
                sp.wait_ge(s_y_sent[n], 16 * (TILES // Y_SLOTS))
            pairs = pair_rows[:].rearrange("(b j p k) d -> b p j k d", b=B, p=P, k=K)
            results = out.rearrange("b (j p) d -> b p j d", p=P)

            def load_pairs(b, par):
                sp.dma_start(pairs_in[par][:], pairs[bass.ds(b, 1)].rearrange(
                    "o p j k d -> (o p) j k d")).then_inc(s_pairs_in[par], 16)

            def store(b):
                sp.wait_ge(d["out"], b + 1)
                sp.dma_start(results[bass.ds(b, 1)].rearrange("o p j d -> (o p) j d"),
                             tiles_of(x, b)).then_inc(s_out, 16)

            for b in (0, 1):
                load_pairs(b, b)
            with sp.Fori(2, B - 1, 2) as b:
                for r in (0, 1):
                    sp.wait_ge(d["moe"], b + (r - 1))
                    load_pairs(b + r, r)
                for r in (0, 1):
                    store(b + (r - 2))
            for b in (B - 2, B - 1):
                store(b)
            sp.wait_ge(s_out, 16 * B)

        @block.gpsimd
        def _(pool):
            pool.memset(ident[:], 0.0)
            pool.memset(before_b[:], 1.0)
            pool.memset(ones_f[:], 1.0)
            pool.memset(ones_b[:], 1.0)
            pool.memset(pad_row[:], 0.0).then_inc(s_pool_step, 1)
            pool.wait_ge(s_pool_step, 1)
            pool.affine_select(out=ident[:], in_=ident[:], compare_op=ALU.not_equal, fill=1.0,
                               base=0, pattern=[[-1, P]], channel_multiplier=1)
            pool.affine_select(out=before_b[:], in_=before_b[:], compare_op=ALU.is_gt, fill=0.0,
                               base=0, pattern=[[1, P]], channel_multiplier=-1)
            pool.memset(pad_row[:, D:D + 1], float(NO_PAIR))
            pool.iota(expert_i[:], pattern=[[1, E]], base=0, channel_multiplier=0)
            pool.iota(token2_i[:], pattern=[[2 * P, B * G]], base=0, channel_multiplier=2)
            pool.iota(tile_i[:], pattern=[[1, TILES]], base=0,
                      channel_multiplier=0).then_inc(s_pool_const, 1)
            pool.wait_ge(s_pool_const, 1)
            for n in range(SPARE):
                first = E * REGION + n * P
                pool.dma_start(expert_rows[first:first + P, :], pad_row[:]).then_inc(s_sent[1], 16)

            def a_round(i, par):
                b = i - 2
                if in_range(b, B):
                    wait_apart(pool, a["place"], b + 1)
                    for j in range(G):
                        for k in range(K):
                            pool.indirect_dma_start(
                                expert_rows[:, :],
                                bass.IndirectOffsetOnAxis(ap=place[par][:, k, j:j + 1], axis=0),
                                row[par][:, j, :], None).then_inc(s_sent[par], 16)

            rounds_of_batches(pool, a_round)

            def c_round(base, r):
                t = base + (r - 3)
                if in_range(t, TILES):
                    slot = (r - 3) % Y_SLOTS
                    wait_apart(pool, c["y"], t + 1)
                    pool.indirect_dma_start(
                        pair_rows[:, :], bass.IndirectOffsetOnAxis(ap=y_pair[slot][:, 0:1], axis=0),
                        y_rows[slot][:], None, bounds_check=T * K - 1,
                        oob_is_err=False).then_inc(s_y_sent[slot], 16)

            rounds_of_tiles(pool, c_round)

        @block.scalar
        def _(act):
            act.dma_start(w_in[:], w_in_in).then_inc(s_small, 16)
            act.dma_start(w_out[:], w_out_in).then_inc(s_small, 16)
            act.dma_start(gate[:], gate_in).then_inc(s_small, 16)
            act.dma_start(b_in[:], b_in_in.rearrange("(p o) -> p o", o=1)).then_inc(s_small, 16)
            for j in range(G):
                act.dma_start(b_out4[0:1, j, :],
                              b_out_in.rearrange("(o n) -> o n", o=1)).then_inc(s_small, 16)
            for to, of in ((decay, decay_in), (mix, mix_in)):
                act.dma_start(to[:], of.rearrange("(o n) -> o n", o=1).broadcast_to(
                    [P, 1])).then_inc(s_small, 16)
            act.wait_ge(s_const, 1)

            def root(sd, mv, b, name_in, name_out):
                act.wait_ge(a[name_in], b + 1)
                act.activation(sd[:], mv[:, :, 1], ACT.Sqrt, bias=eps[:]).then_inc(a[name_out], 1)

            def a_round(i, par):
                b = i - 2
                if in_range(b, B):
                    act.wait_ge(a["xn2T_ps"], b + 1)
                    act.activation(xn2T[par][:], p_xn2T[:], ACT.Copy).then_inc(a["xn2T"], 1)
                if in_range(i, B):
                    root(sd1[par], mv1[par], i, "mv1", "sd1")
                b = i - 1
                if in_range(b, B):
                    root(sd2[1 - par], mv2[1 - par], b, "mv2", "sd2")
                if in_range(i, B):
                    act.wait_ge(a["xn1T_ps"], i + 1)
                    act.activation(shifted[par][:, 1:S], p_xn1T[:, 0:S - 1], ACT.Copy,
                                   scale=one_minus_mix[:]).then_inc(a["shifted"], 1)
                if in_range(b, B):
                    act.wait_ge(a["nm2"], b + 1)
                    for j in range(G):
                        last = act.activation(
                            normed2[1 - par][:, j, :], p_attn[:, j * D:(j + 1) * D], ACT.Identity,
                            scale=rs2[1 - par][:, j:j + 1], bias=nm2[1 - par][:, j:j + 1])
                    last.then_inc(a["normed2"], 1)
                if in_range(i, B):
                    act.wait_ge(a["hidden_ps"], i + 1)
                    act.activation(hidden[par][:], p_hidden[:], ACT.Relu,
                                   bias=b_in[:]).then_inc(a["hidden"], 1)
                if in_range(b, B):
                    root(sd3[1 - par], mv3[1 - par], b, "mv3", "sd3")

            rounds_of_batches(act, a_round)

            act.wait_ge(a["row_done"], B)
            act.activation(weight[:, 1, :], logit_gap[:], ACT.Exp).then_inc(s_exp, 1)

            def c_round(base, r):
                t = base + (r - 1)
                if in_range(t, TILES):
                    act.wait_ge(c["l1_ps"], t + 1)
                    act.activation(silu[(r - 1) % 2][:], p_l1[:],
                                   ACT.Silu).then_inc(c["silu"], 1)
                t = base + (r - 2)
                if in_range(t, TILES):
                    act.wait_ge(c["gatedT_ps"], t + 1)
                    act.activation(gatedT[r % 2][:], p_gatedT[:],
                                   ACT.Copy).then_inc(c["gatedT"], 1)
                t = base + r
                if in_range(t, TILES):
                    act.wait_ge(c["xeT_ps"], t + 1)
                    act.activation(xeT[r % 2][:], p_xeT[:, 0:P], ACT.Copy).then_inc(c["xeT"], 1)

            rounds_of_tiles(act, c_round)

            def weigh_first(b, par):
                act.wait_ge(s_pairs_in[par], 8 * (b - par) + 16)
                for j in range(G):
                    last = act.activation(first_part[par][:, j, :], pairs_in[par][:, j, 0, :],
                                          ACT.Copy, scale=weight[:, 0, bass.ds(b * G + j, 1)])
                last.then_inc(d["first"], 1)

            def d_round(i, par):
                if in_range(i, B):
                    weigh_first(i, par)
                    act.wait_ge(d["mv"], i + 1)
                    act.activation(sd4[par][:], mv4[par][:, :, 1], ACT.Sqrt,
                                   bias=eps[:]).then_inc(d["sd"], 1)
                b = i - 1
                if in_range(b, B):
                    act.wait_ge(d["nm"], b + 1)
                    for j in range(G):
                        last = act.activation(
                            normed4[1 - par][:, j, :], moe[1 - par][:, j, :], ACT.Identity,
                            scale=rs4[1 - par][:, j:j + 1], bias=nm4[1 - par][:, j:j + 1])
                    last.then_inc(d["normed"], 1)

            rounds_of_batches(act, d_round)

        @block.vector
        def _(dve):
            dve.memset(eps[:], EPS)
            for par in (0, 1):
                dve.memset(shifted[par][:, 0:1], 0.0)
            dve.memset(taken[0][:, G, :], 0.0)
            dve.wait_ge(s_pool_const, 1)
            dve.tensor_copy(expert_f[:], expert_i[:])
            dve.tensor_scalar(region_f[:], expert_i[:], float(REGION), None, ALU.mult)
            dve.tensor_copy(token2_f[:], token2_i[:])
            dve.tensor_copy(tile_f[:], tile_i[:])
            dve.wait_ge(s_small, 16 * (4 + G + 2))
            dve.tensor_scalar(decay_row[:].rearrange("p (j n) -> p j n", j=G),
                              ones_f[:, None, :].broadcast_to([P, G, P]), decay[:], None, ALU.mult)
            dve.tensor_scalar(one_minus_mix[:], mix[:], -1.0, 1.0, ALU.mult,
                              ALU.add).then_inc(s_const, 1)
            dve.wait_ge(s_const, 1)
            dve.wait_ge(s_wT_ps, 1)
            dve.tensor_copy(w_inT[:], p_hidden[:, 0:D])
            dve.tensor_copy(w_outT[:], p_hidden[:, D:2 * D]).then_inc(s_wT, 1)

            def row_stats(stats, mv, rows, b, s_stats, s_mv):
                for j in range(G):
                    last = dve.bn_stats(stats[:, j, :], rows(j))
                last.then_inc(s_stats, 1)
                wait_apart(dve, s_stats, b + 1)
                for j in range(G):
                    last = dve.bn_aggr(mv[:, j, :], stats[:, j, :])
                last.then_inc(s_mv, 1)

            def inverse(rs, sd, b, s_sd, s_rs):
                dve.wait_ge(s_sd, b + 1)
                dve.reciprocal(rs[:], sd[:]).then_inc(s_rs, 1)
                dve.wait_ge(s_rs, b + 1)

            def minus_mean_over_sd(nm, mv, rs, s_nm):
                dve.scalar_tensor_tensor(out=nm[:], in0=mv[:, :, 0], scalar=-1.0, in1=rs[:],
                                         op0=ALU.mult, op1=ALU.mult).then_inc(s_nm, 1)

            def normalise(to, of, mv, rs, s_done):
                for j in range(G):
                    last = dve.tensor_scalar(to(j), of(j), mv[:, j, 0:1], rs[:, j:j + 1],
                                             ALU.subtract, ALU.mult)
                last.then_inc(s_done, 1)

            def x_tile(b):
                return lambda j: x[:, bass.ds(b * G + j, 1), :].rearrange("p o d -> p (o d)")

            def a_round(i, par):
                now, one, two = i, i - 1, i - 2
                p1 = 1 - par
                if in_range(now, B):
                    if isinstance(i, int):
                        dve.wait_ge((s_x0, s_x1)[i], 16)
                    row_stats(stats1[par], mv1[par], x_tile(now), now, a["stats1"], a["mv1"])
                if in_range(one, B):
                    wait_apart(dve, a["attn_ps"], one + 1)
                    row_stats(stats2[p1], mv2[p1], lambda j: p_attn[:, j * D:(j + 1) * D], one,
                              a["stats2"], a["mv2"])
                if in_range(now, B):
                    inverse(rs1[par], sd1[par], now, a["sd1"], a["rs1"])
                    normalise(lambda j: xn1[par][:, j, :], x_tile(now), mv1[par], rs1[par],
                              a["xn1"])
                if in_range(one, B):
                    inverse(rs2[p1], sd2[p1], one, a["sd2"], a["rs2"])
                    minus_mean_over_sd(nm2[p1], mv2[p1], rs2[p1], a["nm2"])
                if in_range(two, B):
                    choose(two, par)
                if in_range(now, B):
                    dve.wait_ge(a["shifted"], now + 1)
                    dve.scalar_tensor_tensor(out=mixed[par][:], in0=p_xn1T[:], scalar=mix[:],
                                             in1=shifted[par][:], op0=ALU.mult,
                                             op1=ALU.add).then_inc(a["mixed"], 1)
                if in_range(one, B):
                    dve.wait_ge(a["normed2"], one + 1)
                    dve.tensor_tensor(tiles_of(x, one), tiles_of(x, one), normed2[p1][:],
                                      ALU.add).then_inc(a["x1"], 1)
                    wait_apart(dve, a["x1"], one + 1)
                    row_stats(stats3[p1], mv3[p1], x_tile(one), one, a["stats3"], a["mv3"])
                if in_range(now, B):
                    dve.wait_ge(a["hidden"], now + 1)
                    dve.tensor_tensor_scan(states[par][:], decay_row[:], hidden[par][:], 0.0,
                                           ALU.mult, ALU.add).then_inc(a["states"], 1)
                if in_range(one, B):
                    inverse(rs3[p1], sd3[p1], one, a["sd3"], a["rs3"])
                    if p1:
                        wait(dve, s_sent[1], 8 * K * G * (one - 1) + 16 * SPARE)
                    else:
                        wait(dve, s_sent[0], 8 * K * G * one)
                    normalise(lambda j: row[p1][:, j, 0:D], x_tile(one), mv3[p1], rs3[p1],
                              a["xn2"])
                if in_range(two, B):
                    find_places(two, par)

            def choose(b, par):
                wait_apart(dve, a["gate_ps"], b + 1)
                logits = p_gate[:, 0:G * E].rearrange("p (j e) -> p j e", j=G)
                for j in range(G):
                    last = dve.max(top8[par][:, j, :], logits[:, j, :])
                last.then_inc(a["top8"], 1)
                wait_apart(dve, a["top8"], b + 1)
                for j in range(G):
                    last = dve.max_index(choice8[par][:, j, :], top8[par][:, j, :],
                                         logits[:, j, :])
                last.then_inc(a["choice"], 1)
                dve.tensor_tensor(logit_gap[:, bass.ds(b * G, G)], top8[par][:, :, 1],
                                  top8[par][:, :, 0], ALU.subtract)
                dve.wait_ge(a["choice"], b + 1)
                dve.tensor_copy(choice_f[par][:],
                                choice8[par][:, :, 0:K].rearrange("p j k -> p k j")
                                ).then_inc(a["row_done"], 1)
                dve.wait_ge(a["row_done"], b + 1)
                dve.tensor_tensor(
                    onehot[par][:].rearrange("p k j e -> p (k j) e"),
                    expert_f[:, None, :].broadcast_to([P, K * G, E]),
                    choice_f[par][:].rearrange("p k j -> p (k j)")[:, :, None].broadcast_to(
                        [P, K * G, E]), ALU.is_equal).then_inc(a["onehot"], 1)
                dve.tensor_copy(row[par][:, :, D + 1], choice_f[par][:, 0, :])
                dve.tensor_copy(row[par][:, :, D], token2_f[:, bass.ds(b * G, G)])
                dve.wait_ge(a["onehot"], b + 1)
                dve.tensor_tensor(taken[par][:, 0:G, :], onehot[par][:, 0], onehot[par][:, 1],
                                  ALU.add).then_inc(a["taken"], 1)
                dve.wait_ge(a["taken"], b + 1)
                with nc.allow_low_precision("whole numbers up to 32"):
                    dve.tensor_reduce(taken[1 - par][:, G, :],
                                      taken[par][:].rearrange("p j e -> p e j"), axis=AX.X,
                                      op=ALU.add).then_inc(a["total"], 1)

            def find_places(b, par):
                dve.wait_ge(a["rank_ps"], b + 1)
                dve.tensor_tensor(rank_f[par][:],
                                  p_rank[:, 0:G * E].rearrange("p (j e) -> p j e", j=G),
                                  region_f[:, None, :].broadcast_to([P, G, E]),
                                  ALU.add).then_inc(a["rank"], 1)
                dve.wait_ge(a["rank"], b + 1)
                for k in range(K):
                    last = dve.tensor_tensor(place4[par][:, k], onehot[par][:, k], rank_f[par][:],
                                             ALU.mult)
                last.then_inc(a["place4"], 1)
                dve.wait_ge(a["place4"], b + 1)
                with nc.allow_low_precision("whole numbers below 2 ** 24"):
                    dve.tensor_reduce(place[par][:], place4[par][:], axis=AX.X,
                                      op=ALU.add).then_inc(a["place"], 1)

            for i in (0, 1):
                a_round(i, i)
            dve.wait_ge(s_x2, 16)
            with dve.Fori(2, B - 1, 2) as i:
                for r in (0, 1):
                    a_round(i + r, r)
            for i in (B, B + 1):
                a_round(i, i % 2)

            steps = [0]

            def step(ins):
                steps[0] += 1
                ins.then_inc(s_b, 1)
                dve.wait_ge(s_b, steps[0])

            dve.wait_ge(s_count_ps, 1)
            dve.tensor_tensor(pad_start_i[:], p_rank[:, 0:E], region_f[:], ALU.add)
            step(dve.tensor_scalar(count_i[:], p_rank[:, 0:E], float(P - 1), None, ALU.add))
            step(dve.tensor_scalar(tiles_i[:], count_i[:], P.bit_length() - 1, None,
                                   ALU.arith_shift_right))
            step(dve.tensor_copy(tiles_f[:], tiles_i[:]))
            step(dve.tensor_tensor_scan(ends[:], ones_f[:, 0:E], tiles_f[:], 0.0, ALU.mult,
                                        ALU.add))
            dve.tensor_scalar(skip[:], tiles_f[:], -float(P), float(REGION), ALU.mult, ALU.add)
            step(dve.tensor_tensor(past[:], tile_f[:, :, None].broadcast_to([P, TILES, E]),
                                   ends[:, None, :].broadcast_to([P, TILES, E]), ALU.is_ge))
            dve.tensor_reduce(tile_expert[:], past[:], axis=AX.X, op=ALU.add)
            step(dve.tensor_tensor(past_skip[:], past[:],
                                   skip[:, None, :].broadcast_to([P, TILES, E]), ALU.mult))
            step(dve.tensor_reduce(tile_row[:], past_skip[:], axis=AX.X, op=ALU.add))
            dve.tensor_scalar(tile_column_i[:], tile_expert[:], float(E - 1), float(F), ALU.min,
                              ALU.mult)
            dve.scalar_tensor_tensor(out=tile_row_i[:], in0=tile_f[:], scalar=float(P),
                                     in1=tile_row[:], op0=ALU.mult,
                                     op1=ALU.add).then_inc(s_table, 1)
            dve.wait_ge(s_exp, 1)
            step(dve.tensor_scalar(denom[:], weight[:, 1, :], 1.0, None, ALU.add))
            step(dve.reciprocal(weight[:, 0, :], denom[:]))
            step(dve.tensor_tensor(weight[:, 1, :], weight[:, 1, :], weight[:, 0, :], ALU.mult))

            def c_round(base, r):
                t = base + (r - 1)
                if in_range(t, TILES):
                    dve.wait_ge(c["silu"], t + 1)
                    dve.wait_ge(c["l2_ps"], t + 1)
                    dve.tensor_tensor(gated[(r - 1) % 2][:], p_l2[:], silu[(r - 1) % 2][:],
                                      ALU.mult).then_inc(c["gated"], 1)
                t = base + (r - 3)
                if in_range(t, TILES):
                    slot = (r - 3) % Y_SLOTS
                    dve.wait_ge(c["y_ps"], t + 1)
                    wait(dve, s_y_sent[slot],
                         (16 // Y_SLOTS) * base + 16 * ((r - 3) // Y_SLOTS))
                    source = taken_rows[(r - 3) % UNROLL]
                    dve.scalar_tensor_tensor(
                        out=y_pair[slot][:], in0=source[:, D + 1:D + 2],
                        scalar=tile_expert[:, bass.ds(t, 1)], in1=source[:, D:D + 1],
                        op0=ALU.not_equal, op1=ALU.add)
                    dve.tensor_copy(y_rows[slot][:], p_y[:, 0:D]).then_inc(c["y"], 1)

            rounds_of_tiles(dve, c_round)

            def d_round(i, par):
                one, two = i - 1, i - 2
                if in_range(i, B):
                    dve.wait_ge(d["first"], i + 1)
                    wait(dve, d["normed"], i - 1)
                    for j in range(G):
                        last = dve.scalar_tensor_tensor(
                            out=moe[par][:, j, :], in0=pairs_in[par][:, j, 1, :],
                            scalar=weight[:, 1, bass.ds(i * G + j, 1)],
                            in1=first_part[par][:, j, :], op0=ALU.mult, op1=ALU.add)
                    last.then_inc(d["moe"], 1)
                    wait_apart(dve, d["moe"], i + 1)
                    row_stats(stats4[par], mv4[par], lambda j: moe[par][:, j, :], i, d["stats"],
                              d["mv"])
                if in_range(one, B):
                    inverse(rs4[1 - par], sd4[1 - par], one, d["sd"], d["rs"])
                    minus_mean_over_sd(nm4[1 - par], mv4[1 - par], rs4[1 - par], d["nm"])
                if in_range(two, B):
                    dve.wait_ge(d["normed"], two + 1)
                    dve.tensor_tensor(tiles_of(x, two), tiles_of(x, two), normed4[par][:],
                                      ALU.add).then_inc(d["out"], 1)

            rounds_of_batches(dve, d_round)

        @block.tensor
        def _(pe):
            pe.wait_ge(s_pool_const, 1)
            pe.wait_ge(s_small, 16 * (4 + G + 2))
            pe.transpose(p_hidden[:, 0:D], w_in[:], ident[:])
            pe.transpose(p_hidden[:, D:2 * D], w_out[:], ident[:]).then_inc(s_wT_ps, 1)
            pe.wait_ge(s_wT, 1)

            def a_round(i, par):
                b = i - 2
                if in_range(b, B):
                    pe.wait_ge(a["xn2"], b + 1)
                    for j in range(G):
                        last = pe.transpose(p_xn2T[:, j * P:(j + 1) * P], row[par][:, j, 0:D],
                                            ident[:])
                    last.then_inc(a["xn2T_ps"], 1)
                    pe.wait_ge(a["xn2T"], b + 1)
                    for j in range(G):
                        last = pe.matmul(p_gate[:, j * E:(j + 1) * E],
                                         xn2T[par][:, j * P:(j + 1) * P], gate[:], start=True,
                                         stop=True)
                    last.then_inc(a["gate_ps"], 1)
                if in_range(i, B):
                    pe.wait_ge(a["xn1"], i + 1)
                    for j in range(G):
                        last = pe.transpose(p_xn1T[:, j * P:(j + 1) * P], xn1[par][:, j, :],
                                            ident[:])
                    last.then_inc(a["xn1T_ps"], 1)
                if in_range(b, B):
                    pe.wait_ge(a["total"], b + 1)
                    pe.matmul(p_rank[:, 0:G * E], before_b[:],
                              taken[par][:, 0:G, :].rearrange("p j e -> p (j e)"), start=True,
                              stop=False)
                    for j in range(G - 1):
                        pe.matmul(p_rank[:, (j + 1) * E:G * E], ones_b[:],
                                  taken[par][:, j:j + 1, :].broadcast_to([P, G - 1 - j, E]),
                                  start=False, stop=False)
                    pe.matmul(p_rank[:, 0:G * E], ones_b[:],
                              taken[par][:, G:G + 1, :].broadcast_to([P, G, E]), start=False,
                              stop=True).then_inc(a["rank_ps"], 1)
                if in_range(i, B):
                    pe.wait_ge(a["mixed"], i + 1)
                    pe.matmul(p_hidden[:], w_inT[:], mixed[par][:], start=True,
                              stop=True).then_inc(a["hidden_ps"], 1)
                    pe.wait_ge(a["states"], i + 1)
                    pe.matmul(p_attn[:], ones_f[0:1, :],
                              b_out4[:].rearrange("o j n -> o (j n)"), start=True, stop=False)
                    for j in range(G):
                        last = pe.matmul(p_attn[:, j * D:(j + 1) * D],
                                         states[par][:, j * P:(j + 1) * P], w_outT[:],
                                         start=False, stop=(j == G - 1))
                    last.then_inc(a["attn_ps"], 1)

            rounds_of_batches(pe, a_round)

            pe.wait_ge(a["place"], B)
            pe.matmul(p_rank[:, 0:E], ones_b[:], taken[B % 2][:, G, :], start=True,
                      stop=True).then_inc(s_count_ps, 1)

            pe.wait_ge(s_table, 1)
            pe.wait_ge(s_experts_in, 16 * 3)

            def column_of(t):
                return pe.value_load(tile_column_i[0:1, bass.ds(t, 1)], min_val=0,
                                     max_val=(E - 1) * F)

            def c_round(base, r):
                t = base + (r - 1)
                if in_range(t, TILES):
                    column = column_of(t)
                    pe.wait_ge(c["xeT"], t + 1)
                    wait(pe, c["silu"], t)
                    pe.matmul(p_l1[:], xeT[(r - 1) % 2][:], w0[:, bass.ds(column, F)],
                              start=True, stop=True).then_inc(c["l1_ps"], 1)
                    wait(pe, c["gated"], t)
                    pe.matmul(p_l2[:], xeT[(r - 1) % 2][:], w1[:, bass.ds(column, F)],
                              start=True, stop=True).then_inc(c["l2_ps"], 1)
                t = base + (r - 2)
                if in_range(t, TILES):
                    pe.wait_ge(c["gated"], t + 1)
                    wait(pe, c["gatedT"], t)
                    for n in range(FC):
                        last = pe.transpose(p_gatedT[:, n * P:(n + 1) * P],
                                            gated[r % 2][:, n * P:(n + 1) * P], ident[:])
                    last.then_inc(c["gatedT_ps"], 1)
                t = base + (r - 3)
                if in_range(t, TILES):
                    column = column_of(t)
                    pe.wait_ge(c["gatedT"], t + 1)
                    wait(pe, c["y"], t)
                    for n in range(FC):
                        last = pe.matmul(p_y[:, 0:D],
                                         gatedT[(r - 3) % 2][:, n * P:(n + 1) * P],
                                         wo[:, bass.ds(column + n * D, D)], start=(n == 0),
                                         stop=(n == FC - 1))
                    last.then_inc(c["y_ps"], 1)
                t = base + r
                if in_range(t, TILES):
                    pe.wait_ge(s_rows_in[r % UNROLL],
                               (16 // UNROLL) * base + 16 * (r // UNROLL + 1))
                    pe.transpose(p_xeT[:, 0:P], taken_rows[r % UNROLL][:, 0:D],
                                 ident[:]).then_inc(c["xeT_ps"], 1)

            rounds_of_tiles(pe, c_round)


_INS = ["L0_attn_x", "L0_attn_W_in", "L0_attn_b_in", "L0_attn_W_out", "L0_attn_b_out",
        "L0_attn_decay", "L0_attn_mix", "L0_ffn_gate_kernel", "L0_ffn_w0", "L0_ffn_w1",
        "L0_ffn_wo"]


def kernel(**inputs):
    import numpy as np
    import concourse.bacc as bacc
    from concourse import mybir as _mybir
    from concourse.bass_utils import run_bass_kernel_spmd

    nc = bacc.Bacc("TRN2", target_bir_lowering=False, num_devices=1)
    arrays, args = {}, []
    for name in _INS:
        array = np.ascontiguousarray(inputs[name]).reshape(np.shape(inputs[name]) or (1,))
        arrays["in_" + name] = array
        args.append(nc.dram_tensor("in_" + name, array.shape, _mybir.dt.from_np(array.dtype),
                                   kind="ExternalInput").ap())
    out = nc.dram_tensor("out_dram", (B, S, D), F32, kind="ExternalOutput").ap()
    sandwich_kernel(nc, *args, out)
    r = run_bass_kernel_spmd(nc, [arrays], core_ids=[0])
    return r.results[0]["out_dram"]
```

```python
from contextlib import ExitStack

import concourse.bass as bass
from concourse import mybir

F32 = mybir.dt.float32
F32R = mybir.dt.float32r
BF16 = mybir.dt.bfloat16
I32 = mybir.dt.int32
U32 = mybir.dt.uint32
ALU = mybir.AluOpType
ACT = mybir.ActivationFunctionType
AX = mybir.AxisListType

P = 128
B, S, D = 8, 512, 128
E, F, K = 8, 512, 2
T = B * S
G = S // P
FC = F // P
EPS = 1e-5
REGION = T + P
ROW = D + 2
UNROLL = 8
TILES = -(-(T * K // P + E - 1) // UNROLL) * UNROLL
SPARE = TILES - T * K // P
NO_PAIR = 2 * K * T
WCOLS = E * F
W_CHUNKS = WCOLS // D
BIAS_ROWS = 96
Y_SLOTS = 4


def sandwich_kernel(nc, x_in, w_in_in, b_in_in, w_out_in, b_out_in, decay_in, mix_in,
                    gate_in, w0_in, w1_in, wo_in, out):
    ctx = ExitStack()
    with ctx:
        def sb(name, shape, dt=F32):
            return ctx.enter_context(nc.sbuf_tensor("sb_" + name, shape, dt))

        def sem(name):
            return ctx.enter_context(nc.semaphore(name))

        def pair(name, shape, dt=F32):
            return [sb(f"{name}{n}", shape, dt) for n in range(2)]

        expert_rows = nc.dram_tensor("expert_rows", [E * REGION + SPARE * P, ROW], F32)
        pair_rows = nc.dram_tensor("pair_rows", [T * K, D], F32)

        x = sb("x", [P, B * G, D])
        w_raw = sb("w_raw", [P, 3 * WCOLS])
        w_raw_chunks = w_raw[:].rearrange("p (c d) -> p c d", d=D)
        w_parts = sb("w_parts", [P, 3 * W_CHUNKS, 2, D], F32R)
        w_in = sb("w_in", [P, D])
        w_out = sb("w_out", [P, D])
        w_inT = sb("w_inT", [P, D])
        w_outT = sb("w_outT", [P, D])
        gate = sb("gate", [P, E])
        b_in = sb("b_in", [P, 1])
        b_rows = sb("b_rows", [BIAS_ROWS, D])
        b_rest = sb("b_rest", [BIAS_ROWS, D])
        b_rest2 = sb("b_rest2", [BIAS_ROWS, D])
        b_part = [sb(f"b_part{n}", [BIAS_ROWS, D], BF16) for n in range(3)]
        b_parts = sb("b_parts", [BIAS_ROWS, D], BF16)
        decay = sb("decay", [P, 1])
        mix = sb("mix", [P, 1])
        one_minus_mix = sb("one_minus_mix", [P, 1])
        decay_row = sb("decay_row", [P, S])
        ident = sb("ident", [P, P])
        ones_f = sb("ones_f", [P, P])
        ones_b = sb("ones_b", [P, P], BF16)
        before_b = sb("before_b", [P, P], BF16)
        eps = sb("eps", [P, 1])
        unused = sb("unused", [P, 1])
        expert_i = sb("expert_i", [P, E], I32)
        expert_f = sb("expert_f", [P, E])
        region_f = sb("region_f", [P, E])
        token2_i = sb("token2_i", [P, B * G], I32)
        token2_f = sb("token2_f", [P, B * G])
        tile_i = sb("tile_i", [P, TILES], I32)
        tile_f = sb("tile_f", [P, TILES])
        pad_row = sb("pad_row", [P, ROW])

        stats1, stats2, stats3 = (pair(f"stats{n}_", [P, G, 6]) for n in (1, 2, 3))
        mv1, mv2, mv3 = (pair(f"mv{n}_", [P, G, 2]) for n in (1, 2, 3))
        sd1, sd2, sd3 = (pair(f"sd{n}_", [P, G]) for n in (1, 2, 3))
        rs1, rs2, rs3 = (pair(f"rs{n}_", [P, G]) for n in (1, 2, 3))
        nm1, nm2, nm3 = (pair(f"nm{n}_", [P, G]) for n in (1, 2, 3))
        early = sb("early", [P, 4 * S])
        mixed, hidden, xn1_flat, shifted = (early[:, n * S:(n + 1) * S] for n in range(4))
        xn1 = xn1_flat.rearrange("p (j d) -> p j d", j=G)
        states = sb("states", [P, S])
        normed2 = sb("normed2", [P, G, D])
        row = pair("row", [P, G, ROW])
        xn2T = sb("xn2T", [P, S])
        top8 = pair("top8_", [P, G, 8])
        choice8 = pair("choice8_", [P, G, 8], U32)
        choice_f = pair("choice_f", [P, K, G])
        onehot = pair("onehot", [P, K, G, E], BF16)
        taken = pair("taken", [P, G + 1, E], BF16)
        rank_f = pair("rank_f", [P, G, E])
        place4 = pair("place4_", [P, K, G, E])
        place = pair("place", [P, K, G], I32)
        logit_gap = sb("logit_gap", [P, B * G])
        weight = sb("weight", [P, K, B * G])
        denom = sb("denom", [P, B * G])
        weight0_square = sb("weight0_square", [P, B * G])

        count = sb("count", [P, E])
        count_i = sb("count_i", [P, E], I32)
        tiles_i = sb("tiles_i", [P, E], I32)
        tiles_f = sb("tiles_f", [P, E])
        ends = sb("ends", [P, E])
        skip = sb("skip", [P, E])
        past, past_skip = (early[:, n * TILES * E:(n + 1) * TILES * E].rearrange(
            "p (t e) -> p t e", t=TILES) for n in (0, 1))
        tile_expert = sb("tile_expert", [P, TILES])
        tile_chunk_i = sb("tile_chunk_i", [P, TILES], I32)
        tile_row = sb("tile_row", [P, TILES])
        tile_row_i = sb("tile_row_i", [P, TILES], I32)
        pad_start = sb("pad_start", [P, E])
        pad_start_i = sb("pad_start_i", [P, E], I32)

        taken_rows = [early[:, n * ROW:(n + 1) * ROW] for n in range(UNROLL)]
        y_rows = [early[:, UNROLL * ROW + n * D:UNROLL * ROW + (n + 1) * D]
                  for n in range(Y_SLOTS)]
        x_hi, x_lo = pair("x_hi", [P, P], F32R), pair("x_lo", [P, P], F32R)
        g_hi, g_lo = pair("g_hi", [P, F], F32R), pair("g_lo", [P, F], F32R)
        silu = [w_raw[:, n * F:(n + 1) * F] for n in (0, 1)]
        gated = [w_raw[:, n * F:(n + 1) * F] for n in (2, 3)]
        y_pair = [sb(f"y_pair{n}", [P, 1], I32) for n in range(Y_SLOTS)]

        pairs_in = [w_raw[:, 2 * WCOLS + n * G * K * D:2 * WCOLS + (n + 1) * G * K * D].rearrange(
            "p (j k d) -> p j k d", j=G, k=K) for n in (0, 1)]
        moe, normed4 = ([w_raw[:, 2 * WCOLS + n * G * D:2 * WCOLS + (n + 1) * G * D].rearrange(
            "p (j d) -> p j d", j=G) for n in ns] for ns in ((4, 5), (6, 7)))
        scaled_var = pair("scaled_var", [P, G])
        inv4 = pair("inv4_", [P, G])
        stats4, mv4 = pair("stats4_", [P, G, 6]), pair("mv4_", [P, G, 2])
        sd4, rs4, nm4 = pair("sd4_", [P, G]), pair("rs4_", [P, G]), pair("nm4_", [P, G])

        bank = [ctx.enter_context(nc.psum_tensor(f"bank{n}", [P, 512], F32)) for n in range(8)]
        p_xn1T, p_hidden, p_attn, p_xn2T, p_gate, p_rank = bank[:6]
        p_xeT, p_l1, p_l2, p_gatedT = bank[:4]
        p_y = bank[4:6]

        s_x0, s_x1, s_x2 = sem("x_batch0_in"), sem("x_batch1_in"), sem("x_rest_in")
        s_small, s_bias_in = sem("small_in"), sem("bias_in")
        s_w_in = [sem("w0_in"), sem("w1_in"), sem("wo_in")]
        s_w_hi, s_w01_lo, s_wo_lo = sem("w_hi"), sem("w0_w1_lo"), sem("wo_lo")
        s_pool_const, s_pool_step, s_const = sem("pool_const"), sem("pool_step"), sem("const")
        s_wT_ps, s_wT = sem("wT_ps"), sem("wT")
        s_apart = sem("waited_apart")
        names_a = ("stats1 mv1 sd1 rs1 xn1 xn1T_ps shifted mixed hidden_ps hidden states attn_ps "
                   "nm1 nm3 stats2 mv2 sd2 rs2 nm2 normed2 x1 stats3 mv3 sd3 rs3 xn2 xn2T_ps xn2T gate_ps "
                   "gap top8 choice onehot taken total rank_ps rank place4 place row_done")
        a = {n: sem("a_" + n) for n in names_a.split()}
        s_sent = [sem("rows_sent_even"), sem("rows_sent_odd")]
        s_count_ps, s_b, s_table, s_pads = sem("count_ps"), sem("b_step"), sem("table"), sem("pads")
        s_exp = sem("exp")
        names_c = "xeT_ps x_hi x_lo l1_ps l2_ps silu gated gatedT_ps g_hi g_lo y_ps y"
        c = {n: sem("c_" + n) for n in names_c.split()}
        s_rows_in = [sem(f"tile_in{n}") for n in range(UNROLL)]
        s_y_sent = [sem(f"y_sent{n}") for n in range(Y_SLOTS)]
        names_d = "moe stats mv scaled sd inv rs nm normed out"
        d = {n: sem("d_" + n) for n in names_d.split()}
        s_pairs_in = [sem("pairs_in_even"), sem("pairs_in_odd")]
        s_out = sem("out_written")

        def wait(eng, s, value):
            if not (isinstance(value, int) and value <= 0):
                eng.wait_ge(s, value)

        def wait_apart(eng, s, value):
            eng.wait_ge(s, value).then_inc(s_apart, 1)

        def in_range(n, count):
            return not isinstance(n, int) or 0 <= n < count

        def rounds_of_a(eng, a_round):
            for i in (-1, 0, 1):
                a_round(i, i % 2)
            with eng.Fori(2, B - 3, 2) as i:
                for r in (0, 1):
                    a_round(i + r, r)
            for i in range(B - 2, B + 2):
                a_round(i, i % 2)

        def rounds_of_d(eng, a_round):
            for i in (0, 1, 2):
                a_round(i, i % 2)
            with eng.Fori(3, B - 2, 2) as i:
                for r in (0, 1):
                    a_round(i + r, 1 - r)
            for i in (B - 1, B):
                a_round(i, i % 2)

        def rounds_of_tiles(eng, a_round):
            for k in range(UNROLL):
                a_round(0, k)
            with eng.Fori(UNROLL, TILES - UNROLL + 1, UNROLL) as base:
                for r in range(UNROLL):
                    a_round(base, r)
            for k in range(3):
                a_round(TILES, k)

        def x_tile(b):
            return lambda j: x[:, bass.ds(b * G + j, 1), :].rearrange("p o d -> p (o d)")

        def tiles_of(t, b):
            return t[:, bass.ds(b * G, G)]

        def pad_experts(eng, first_expert):
            eng.wait_ge(s_b, 2)
            for e in range(first_expert, E, 2):
                first = eng.value_load(pad_start_i[0:1, e:e + 1], min_val=e * REGION,
                                       max_val=e * REGION + T)
                eng.dma_start(expert_rows[bass.ds(first, P), :], pad_row[:]).then_inc(s_pads, 16)

        block = ctx.enter_context(nc.Block())

        @block.sync
        def _(sp):
            tokens = x_in.rearrange("b (j p) d -> p (b j) d", p=P)
            sp.dma_start(x[:, 0:G], tokens[:, 0:G]).then_inc(s_x0, 16)
            sp.dma_start(gate[:], gate_in).then_inc(s_small, 16)
            sp.dma_start(b_rows[:], b_out_in.rearrange("(o n) -> o n", o=1).broadcast_to(
                [BIAS_ROWS, D])).then_inc(s_bias_in, 16)
            sp.dma_start(x[:, G:2 * G], tokens[:, G:2 * G]).then_inc(s_x1, 16)
            sp.wait_ge(s_small, 16 * 6)
            sp.dma_start(x[:, 2 * G:], tokens[:, 2 * G:]).then_inc(s_x2, 16)
            for n, w in enumerate((w0_in, w1_in)):
                sp.dma_start(w_raw[:, n * WCOLS:(n + 1) * WCOLS].rearrange(
                    "p (e f) -> p e f", e=E), w.rearrange("e d f -> d e f")
                             ).then_inc(s_w_in[n], 16)
            sp.dma_start(w_raw[:, 2 * WCOLS:].rearrange("p (e c n) -> p e c n", e=E, c=FC),
                         wo_in.rearrange("e (c p) n -> p e c n", p=P)).then_inc(s_w_in[2], 16)

            pad_experts(sp, 0)
            sp.wait_ge(s_table, 1)

            def first_row(t):
                return sp.value_load(tile_row_i[0:1, bass.ds(t, 1)], min_val=0,
                                     max_val=E * REGION + (SPARE - 1) * P)

            def load_tile(first, r):
                sp.dma_start(taken_rows[r][:],
                             expert_rows[bass.ds(first, P), :]).then_inc(s_rows_in[r], 16)

            ahead = [first_row(r) for r in range(4)]
            sp.wait_ge(s_pads, 16 * E)
            sp.wait_ge(s_sent[0], 16 * K * G * (B // 2))
            sp.wait_ge(s_sent[1], 16 * K * G * (B // 2) + 16 * SPARE)
            for r in range(UNROLL):
                load_tile(ahead[r] if r < len(ahead) else first_row(r), r)
            with sp.Fori(UNROLL, TILES - UNROLL + 1, UNROLL) as base:
                for r in range(UNROLL):
                    sp.wait_ge(c["y"], base + (r - UNROLL + 1))
                    load_tile(first_row(base + r), r)

            for n in range(Y_SLOTS):
                sp.wait_ge(s_y_sent[n], 16 * (TILES // Y_SLOTS))
            pairs = pair_rows[:].rearrange("(b j p k) d -> b p j k d", b=B, p=P, k=K)

            def load_pairs(b, par):
                sp.dma_start(pairs_in[par][:], pairs[bass.ds(b, 1)].rearrange(
                    "o p j k d -> (o p) j k d")).then_inc(s_pairs_in[par], 16)

            for b in (0, 1):
                load_pairs(b, b)
            with sp.Fori(2, B - 1, 2) as b:
                for r in (0, 1):
                    sp.wait_ge(d["moe"], b + (r - 1))
                    load_pairs(b + r, r)

        @block.gpsimd
        def _(pool):
            pool.memset(ident[:], 0.0)
            pool.memset(before_b[:], 1.0)
            pool.memset(ones_f[:], 1.0)
            pool.memset(ones_b[:], 1.0)
            pool.memset(pad_row[:], 0.0).then_inc(s_pool_step, 1)
            pool.wait_ge(s_pool_step, 1)
            pool.affine_select(out=ident[:], in_=ident[:], compare_op=ALU.not_equal, fill=1.0,
                               base=0, pattern=[[-1, P]], channel_multiplier=1)
            pool.affine_select(out=before_b[:], in_=before_b[:], compare_op=ALU.is_gt, fill=0.0,
                               base=0, pattern=[[1, P]], channel_multiplier=-1)
            pool.memset(pad_row[:, D:D + 1], float(NO_PAIR))
            pool.iota(expert_i[:], pattern=[[1, E]], base=0, channel_multiplier=0)
            pool.iota(token2_i[:], pattern=[[2 * P, B * G]], base=0, channel_multiplier=2)
            pool.iota(tile_i[:], pattern=[[1, TILES]], base=0,
                      channel_multiplier=0).then_inc(s_pool_const, 1)
            pool.wait_ge(s_pool_const, 1)
            for n in range(SPARE):
                first = E * REGION + n * P
                pool.dma_start(expert_rows[first:first + P, :], pad_row[:]).then_inc(s_sent[1], 16)

            for n in range(2):
                part = slice(n * W_CHUNKS, (n + 1) * W_CHUNKS)
                pool.wait_ge(s_w_hi, n + 1)
                pool.tensor_tensor(w_parts[:, part, 1, :], w_raw_chunks[:, part],
                                   w_parts[:, part, 0, :].bitcast(F32),
                                   ALU.subtract).then_inc(s_w01_lo, 1)

            def a_round(i, par):
                b = i - 2
                if in_range(b, B):
                    wait_apart(pool, a["place"], b + 1)
                    for j in range(G):
                        for k in range(K):
                            pool.indirect_dma_start(
                                expert_rows[:, :],
                                bass.IndirectOffsetOnAxis(ap=place[par][:, k, j:j + 1], axis=0),
                                row[par][:, j, :], None).then_inc(s_sent[par], 16)

            rounds_of_a(pool, a_round)

            def c_round(base, r):
                t = base + (r - 3)
                if in_range(t, TILES):
                    slot = (r - 3) % Y_SLOTS
                    wait_apart(pool, c["y"], t + 1)
                    pool.indirect_dma_start(
                        pair_rows[:, :], bass.IndirectOffsetOnAxis(ap=y_pair[slot][:, 0:1], axis=0),
                        y_rows[slot][:], None, bounds_check=T * K - 1,
                        oob_is_err=False).then_inc(s_y_sent[slot], 16)

            rounds_of_tiles(pool, c_round)

            results = out.rearrange("b (j p) d -> b p j d", p=P)

            def add(b, par):
                pool.wait_ge(d["normed"], b + 1)
                pool.tensor_tensor(tiles_of(x, b), tiles_of(x, b), normed4[par],
                                   ALU.add).then_inc(d["out"], 1)

            def store(b):
                wait_apart(pool, d["out"], b + 1)
                pool.dma_start(results[bass.ds(b, 1)].rearrange("o p j d -> (o p) j d"),
                               tiles_of(x, b)).then_inc(s_out, 16)

            add(0, 0)
            with pool.Fori(1, B - 2, 2) as b:
                for r in (0, 1):
                    add(b + r, 1 - r)
                    store(b + (r - 1))
            add(B - 1, 1)
            for b in (B - 2, B - 1):
                store(b)
            pool.wait_ge(s_out, 16 * B)

        @block.scalar
        def _(act):
            for to, of in ((decay, decay_in), (mix, mix_in)):
                act.dma_start(to[:], of.rearrange("(o n) -> o n", o=1).broadcast_to(
                    [P, 1])).then_inc(s_small, 16)
            act.dma_start(w_in[:], w_in_in).then_inc(s_small, 16)
            act.dma_start(w_out[:], w_out_in).then_inc(s_small, 16)
            act.dma_start(b_in[:], b_in_in.rearrange("(p o) -> p o", o=1)).then_inc(s_small, 16)
            act.wait_ge(s_const, 1)

            def root(sd, mv, b, name_in, name_out):
                act.wait_ge(a[name_in], b + 1)
                act.activation(sd[:], mv[:, :, 1], ACT.Sqrt, bias=eps[:]).then_inc(a[name_out], 1)

            def normalise(to, of, rs, nm, s_done):
                for j in range(G):
                    last = act.activation(to(j), of(j), ACT.Identity, scale=rs[:, j:j + 1],
                                          bias=nm[:, j:j + 1])
                last.then_inc(s_done, 1)

            def a_round(i, par):
                now, one, two, nxt = i, i - 1, i - 2, i + 1
                p1 = 1 - par
                if in_range(one, B):
                    root(sd2[p1], mv2[p1], one, "mv2", "sd2")
                    act.wait_ge(a["nm2"], one + 1)
                    normalise(lambda j: normed2[:, j, :],
                              lambda j: p_attn[:, j * D:(j + 1) * D], rs2[p1], nm2[p1],
                              a["normed2"])
                if in_range(now, B):
                    act.wait_ge(a["hidden_ps"], now + 1)
                    act.activation(hidden, p_hidden[:], ACT.Relu,
                                   bias=b_in[:]).then_inc(a["hidden"], 1)
                if in_range(nxt, B):
                    root(sd1[p1], mv1[p1], nxt, "mv1", "sd1")
                if in_range(two, B):
                    act.wait_ge(a["xn2T_ps"], two + 1)
                    act.activation(xn2T[:], p_xn2T[:], ACT.Copy).then_inc(a["xn2T"], 1)
                if in_range(nxt, B):
                    act.wait_ge(a["nm1"], nxt + 1)
                    normalise(lambda j: xn1[:, j, :], x_tile(nxt), rs1[p1], nm1[p1],
                              a["xn1"])
                if in_range(one, B):
                    root(sd3[p1], mv3[p1], one, "mv3", "sd3")
                if in_range(nxt, B):
                    if isinstance(nxt, int) and nxt == 0:
                        act.wait_ge(s_const, 2)
                    act.wait_ge(a["xn1T_ps"], nxt + 1)
                    act.activation(shifted[:, 1:S], p_xn1T[:, 0:S - 1], ACT.Copy,
                                   scale=one_minus_mix[:]).then_inc(a["shifted"], 1)
                if in_range(one, B):
                    if p1:
                        wait(act, s_sent[1], 8 * K * G * (one - 1) + 16 * SPARE)
                    else:
                        wait(act, s_sent[0], 8 * K * G * one)
                    act.wait_ge(a["nm3"], one + 1)
                    normalise(lambda j: row[p1][:, j, 0:D], x_tile(one), rs3[p1], nm3[p1],
                              a["xn2"])
                if isinstance(now, int) and now in (0, 1):
                    round_weights(now)

            def round_weights(n):
                part = slice(n * W_CHUNKS, (n + 1) * W_CHUNKS)
                act.wait_ge(s_w_in[n], 16)
                act.activation(w_parts[:, part, 0, :], w_raw_chunks[:, part],
                               ACT.Copy).then_inc(s_w_hi, 1)

            rounds_of_a(act, a_round)
            round_weights(2)
            pad_experts(act, 1)
            act.activation(unused[:], eps[:], ACT.Silu)

            def c_round(base, r):
                t = base + r
                if in_range(t, TILES):
                    act.wait_ge(c["xeT_ps"], t + 1)
                    act.activation(x_hi[r % 2][:], p_xeT[:, 0:P], ACT.Copy).then_inc(c["x_hi"], 1)
                t = base + (r - 1)
                if in_range(t, TILES):
                    act.wait_ge(c["l1_ps"], t + 1)
                    act.activation(silu[(r - 1) % 2][:], p_l1[:],
                                   ACT.Silu).then_inc(c["silu"], 1)
                t = base + (r - 2)
                if in_range(t, TILES):
                    act.wait_ge(c["gatedT_ps"], t + 1)
                    act.activation(g_hi[r % 2][:], p_gatedT[:], ACT.Copy).then_inc(c["g_hi"], 1)

            rounds_of_tiles(act, c_round)

            act.wait_ge(a["gap"], B)
            act.activation(weight[:, 1, :], logit_gap[:], ACT.Exp).then_inc(s_exp, 1)

            def d_round(i, par):
                b = i - 1
                if in_range(b, B):
                    wait(act, d["out"], b - 1)
                    act.wait_ge(d["nm"], b + 1)
                    normalise(lambda j: normed4[1 - par][:, j, :],
                              lambda j: moe[1 - par][:, j, :], rs4[1 - par], nm4[1 - par],
                              d["normed"])
                if in_range(i, B):
                    act.wait_ge(d["scaled"], i + 1)
                    act.activation(sd4[par][:], scaled_var[par][:], ACT.Sqrt,
                                   bias=eps[:]).then_inc(d["sd"], 1)

            rounds_of_d(act, d_round)

        @block.vector
        def _(dve):
            dve.memset(eps[:], EPS)
            dve.memset(shifted[:, 0:1], 0.0)
            dve.memset(b_parts[:], 0.0)
            dve.memset(taken[0][:, G, :], 0.0).then_inc(s_const, 1)

            def constants():
                dve.wait_ge(s_pool_const, 1)
                dve.tensor_copy(expert_f[:], expert_i[:])
                dve.tensor_scalar(region_f[:], expert_i[:], float(REGION), None, ALU.mult)
                dve.tensor_copy(token2_f[:], token2_i[:])
                dve.tensor_copy(tile_f[:], tile_i[:])
                dve.wait_ge(s_small, 16 * 6)
                dve.tensor_scalar(one_minus_mix[:], mix[:], -1.0, 1.0, ALU.mult,
                                  ALU.add).then_inc(s_const, 1)
                dve.tensor_scalar(decay_row[:].rearrange("p (j n) -> p j n", j=G),
                                  ones_f[:, None, :].broadcast_to([P, G, P]), decay[:], None,
                                  ALU.mult)
                dve.wait_ge(s_wT_ps, 1)
                dve.tensor_copy(w_inT[:], p_hidden[:, 0:D])
                dve.tensor_copy(w_outT[:], p_hidden[:, D:2 * D]).then_inc(s_wT, 1)

            def split_bias():
                dve.wait_ge(s_bias_in, 16)
                dve.tensor_copy(b_part[0][:], b_rows[:]).then_inc(s_const, 1)
                dve.wait_ge(s_const, 3)
                dve.tensor_tensor(b_rest[:], b_rows[:], b_part[0][:],
                                  ALU.subtract).then_inc(s_const, 1)
                dve.wait_ge(s_const, 4)
                dve.tensor_copy(b_part[1][:], b_rest[:]).then_inc(s_const, 1)
                dve.wait_ge(s_const, 5)
                dve.tensor_tensor(b_rest2[:], b_rest[:], b_part[1][:],
                                  ALU.subtract).then_inc(s_const, 1)
                dve.wait_ge(s_const, 6)
                dve.tensor_copy(b_part[2][:], b_rest2[:]).then_inc(s_const, 1)
                dve.wait_ge(s_const, 7)
                for n in range(3):
                    last = dve.tensor_copy(b_parts[32 * n:32 * n + 1, :],
                                           b_part[n][32 * n:32 * n + 1, :])
                last.then_inc(s_const, 1)

            def stats(to, rows, s_stats):
                for j in range(G):
                    last = dve.bn_stats(to[:, j, :], rows(j))
                last.then_inc(s_stats, 1)

            def mean_var(mv, of, b, s_stats, s_mv):
                wait_apart(dve, s_stats, b + 1)
                for j in range(G):
                    last = dve.bn_aggr(mv[:, j, :], of[:, j, :])
                last.then_inc(s_mv, 1)

            def minus_mean_over_sd(nm, mv, rs, b, s_rs, s_nm):
                dve.wait_ge(s_rs, b + 1)
                dve.scalar_tensor_tensor(out=nm[:], in0=mv[:, :, 0], scalar=-1.0, in1=rs[:],
                                         op0=ALU.mult, op1=ALU.mult).then_inc(s_nm, 1)

            def a_round(i, par):
                now, one, two, nxt = i, i - 1, i - 2, i + 1
                p1 = 1 - par
                if in_range(one, B):
                    wait_apart(dve, a["attn_ps"], one + 1)
                    stats(stats2[p1], lambda j: p_attn[:, j * D:(j + 1) * D], a["stats2"])
                    mean_var(mv2[p1], stats2[p1], one, a["stats2"], a["mv2"])
                if in_range(now, B):
                    dve.wait_ge(a["shifted"], now + 1)
                    dve.scalar_tensor_tensor(out=mixed, in0=p_xn1T[:], scalar=mix[:],
                                             in1=shifted, op0=ALU.mult,
                                             op1=ALU.add).then_inc(a["mixed"], 1)
                if in_range(one, B):
                    dve.wait_ge(a["sd2"], one + 1)
                    dve.reciprocal(rs2[p1][:], sd2[p1][:]).then_inc(a["rs2"], 1)
                    minus_mean_over_sd(nm2[p1], mv2[p1], rs2[p1], one, a["rs2"], a["nm2"])
                if in_range(nxt, B):
                    if isinstance(nxt, int) and nxt <= 2:
                        dve.wait_ge((s_x0, s_x1, s_x2)[nxt], 16)
                    stats(stats1[p1], x_tile(nxt), a["stats1"])
                    mean_var(mv1[p1], stats1[p1], nxt, a["stats1"], a["mv1"])
                if in_range(one, B):
                    dve.wait_ge(a["normed2"], one + 1)
                    dve.tensor_tensor(tiles_of(x, one), tiles_of(x, one), normed2[:],
                                      ALU.add).then_inc(a["x1"], 1)
                if in_range(nxt, B):
                    dve.wait_ge(a["sd1"], nxt + 1)
                    dve.reciprocal(rs1[p1][:], sd1[p1][:]).then_inc(a["rs1"], 1)
                    minus_mean_over_sd(nm1[p1], mv1[p1], rs1[p1], nxt, a["rs1"], a["nm1"])
                    if isinstance(nxt, int) and nxt == 0:
                        constants()
                if in_range(one, B):
                    wait_apart(dve, a["x1"], one + 1)
                    stats(stats3[p1], x_tile(one), a["stats3"])
                    mean_var(mv3[p1], stats3[p1], one, a["stats3"], a["mv3"])
                if in_range(now, B):
                    if isinstance(now, int) and now == 0:
                        split_bias()
                    dve.wait_ge(a["hidden"], now + 1)
                    dve.tensor_tensor_scan(states[:], decay_row[:], hidden, 0.0,
                                           ALU.mult, ALU.add).then_inc(a["states"], 1)
                if in_range(two, B):
                    top_two(two, par)
                if in_range(one, B):
                    dve.wait_ge(a["sd3"], one + 1)
                    dve.reciprocal(rs3[p1][:], sd3[p1][:]).then_inc(a["rs3"], 1)
                    minus_mean_over_sd(nm3[p1], mv3[p1], rs3[p1], one, a["rs3"], a["nm3"])
                if in_range(two, B):
                    choose(two, par)
                    find_places(two, par)

            def top_two(b, par):
                wait_apart(dve, a["gate_ps"], b + 1)
                logits = p_gate[:, 0:G * E].rearrange("p (j e) -> p j e", j=G)
                for j in range(G):
                    last = dve.max(top8[par][:, j, :], logits[:, j, :])
                last.then_inc(a["top8"], 1)
                wait_apart(dve, a["top8"], b + 1)
                for j in range(G):
                    last = dve.max_index(choice8[par][:, j, :], top8[par][:, j, :],
                                         logits[:, j, :])
                last.then_inc(a["choice"], 1)
                dve.tensor_tensor(logit_gap[:, bass.ds(b * G, G)], top8[par][:, :, 1],
                                  top8[par][:, :, 0], ALU.subtract).then_inc(a["gap"], 1)

            def choose(b, par):
                dve.wait_ge(a["choice"], b + 1)
                dve.tensor_copy(choice_f[par][:],
                                choice8[par][:, :, 0:K].rearrange("p j k -> p k j")
                                ).then_inc(a["row_done"], 1)
                dve.wait_ge(a["row_done"], b + 1)
                dve.tensor_tensor(
                    onehot[par][:].rearrange("p k j e -> p (k j) e"),
                    expert_f[:, None, :].broadcast_to([P, K * G, E]),
                    choice_f[par][:].rearrange("p k j -> p (k j)")[:, :, None].broadcast_to(
                        [P, K * G, E]), ALU.is_equal).then_inc(a["onehot"], 1)
                dve.tensor_copy(row[par][:, :, D + 1], choice_f[par][:, 0, :])
                dve.tensor_copy(row[par][:, :, D], token2_f[:, bass.ds(b * G, G)])
                dve.wait_ge(a["onehot"], b + 1)
                dve.tensor_tensor(taken[par][:, 0:G, :], onehot[par][:, 0], onehot[par][:, 1],
                                  ALU.add).then_inc(a["taken"], 1)
                dve.wait_ge(a["taken"], b + 1)
                with nc.allow_low_precision("whole numbers up to 32"):
                    dve.tensor_reduce(taken[1 - par][:, G, :],
                                      taken[par][:].rearrange("p j e -> p e j"), axis=AX.X,
                                      op=ALU.add).then_inc(a["total"], 1)

            def find_places(b, par):
                dve.wait_ge(a["rank_ps"], b + 1)
                dve.tensor_tensor(rank_f[par][:],
                                  p_rank[:, 0:G * E].rearrange("p (j e) -> p j e", j=G),
                                  region_f[:, None, :].broadcast_to([P, G, E]),
                                  ALU.add).then_inc(a["rank"], 1)
                dve.wait_ge(a["rank"], b + 1)
                for k in range(K):
                    last = dve.tensor_tensor(place4[par][:, k], onehot[par][:, k], rank_f[par][:],
                                             ALU.mult)
                last.then_inc(a["place4"], 1)
                dve.wait_ge(a["place4"], b + 1)
                with nc.allow_low_precision("whole numbers below 2 ** 24"):
                    dve.tensor_reduce(place[par][:], place4[par][:], axis=AX.X,
                                      op=ALU.add).then_inc(a["place"], 1)

            rounds_of_a(dve, a_round)

            steps = [0]

            def step(ins):
                steps[0] += 1
                ins.then_inc(s_b, 1)
                dve.wait_ge(s_b, steps[0])

            dve.wait_ge(s_count_ps, 1)
            dve.tensor_tensor(pad_start_i[:], p_rank[:, 0:E], region_f[:], ALU.add)
            step(dve.tensor_scalar(count_i[:], p_rank[:, 0:E], float(P - 1), None, ALU.add))
            step(dve.tensor_scalar(tiles_i[:], count_i[:], P.bit_length() - 1, None,
                                   ALU.arith_shift_right))
            step(dve.tensor_copy(tiles_f[:], tiles_i[:]))
            step(dve.tensor_tensor_scan(ends[:], ones_f[:, 0:E], tiles_f[:], 0.0, ALU.mult,
                                        ALU.add))
            dve.tensor_scalar(skip[:], tiles_f[:], -float(P), float(REGION), ALU.mult, ALU.add)
            step(dve.tensor_tensor(past[:], tile_f[:, :, None].broadcast_to([P, TILES, E]),
                                   ends[:, None, :].broadcast_to([P, TILES, E]), ALU.is_ge))
            dve.tensor_reduce(tile_expert[:], past[:], axis=AX.X, op=ALU.add)
            step(dve.tensor_tensor(past_skip[:], past[:],
                                   skip[:, None, :].broadcast_to([P, TILES, E]), ALU.mult))
            step(dve.tensor_reduce(tile_row[:], past_skip[:], axis=AX.X, op=ALU.add))
            dve.tensor_scalar(tile_chunk_i[:], tile_expert[:], float(E - 1), float(FC), ALU.min,
                              ALU.mult)
            dve.scalar_tensor_tensor(out=tile_row_i[:], in0=tile_f[:], scalar=float(P),
                                     in1=tile_row[:], op0=ALU.mult,
                                     op1=ALU.add).then_inc(s_table, 1)
            dve.wait_ge(s_w_hi, 3)
            dve.tensor_tensor(w_parts[:, 2 * W_CHUNKS:, 1, :], w_raw_chunks[:, 2 * W_CHUNKS:],
                              w_parts[:, 2 * W_CHUNKS:, 0, :].bitcast(F32),
                              ALU.subtract).then_inc(s_wo_lo, 1)

            def c_round(base, r):
                t = base + r
                if in_range(t, TILES):
                    dve.wait_ge(c["x_hi"], t + 1)
                    dve.tensor_tensor(x_lo[r % 2][:], p_xeT[:, 0:P], x_hi[r % 2][:].bitcast(F32),
                                      ALU.subtract).then_inc(c["x_lo"], 1)
                t = base + (r - 1)
                if in_range(t, TILES):
                    dve.wait_ge(c["silu"], t + 1)
                    dve.wait_ge(c["l2_ps"], t + 1)
                    dve.tensor_tensor(gated[(r - 1) % 2][:], p_l2[:], silu[(r - 1) % 2][:],
                                      ALU.mult).then_inc(c["gated"], 1)
                t = base + (r - 2)
                if in_range(t, TILES):
                    dve.wait_ge(c["g_hi"], t + 1)
                    dve.tensor_tensor(g_lo[r % 2][:], p_gatedT[:], g_hi[r % 2][:].bitcast(F32),
                                      ALU.subtract).then_inc(c["g_lo"], 1)
                t = base + (r - 3)
                if in_range(t, TILES):
                    slot = (r - 3) % Y_SLOTS
                    dve.wait_ge(c["y_ps"], t + 1)
                    wait(dve, s_y_sent[slot],
                         (16 // Y_SLOTS) * base + 16 * ((r - 3) // Y_SLOTS))
                    source = taken_rows[(r - 3) % UNROLL]
                    dve.scalar_tensor_tensor(
                        out=y_pair[slot][:], in0=source[:, D + 1:D + 2],
                        scalar=tile_expert[:, bass.ds(t, 1)], in1=source[:, D:D + 1],
                        op0=ALU.not_equal, op1=ALU.add)
                    half = p_y[(r - 3) % 2]
                    dve.tensor_reduce(y_rows[slot][:],
                                      half[:, 0:2 * D].rearrange("p (h d) -> p d h", h=2),
                                      axis=AX.X, op=ALU.add).then_inc(c["y"], 1)

            rounds_of_tiles(dve, c_round)

            dve.wait_ge(s_exp, 1)
            step(dve.tensor_scalar(denom[:], weight[:, 1, :], 1.0, None, ALU.add))
            step(dve.reciprocal(weight[:, 0, :], denom[:]))
            step(dve.tensor_tensor(weight0_square[:], weight[:, 0, :], weight[:, 0, :], ALU.mult))

            def d_round(i, par):
                one, p1 = i - 1, 1 - par
                if in_range(i, B):
                    dve.wait_ge(s_pairs_in[par], 8 * (i - par) + 16)
                    wait(dve, d["normed"], i - 1)
                    for j in range(G):
                        last = dve.scalar_tensor_tensor(
                            out=moe[par][:, j, :], in0=pairs_in[par][:, j, 1, :],
                            scalar=weight[:, 1, bass.ds(i * G + j, 1)],
                            in1=pairs_in[par][:, j, 0, :], op0=ALU.mult, op1=ALU.add)
                    last.then_inc(d["moe"], 1)
                if in_range(one, B):
                    dve.wait_ge(d["sd"], one + 1)
                    dve.reciprocal(inv4[p1][:], sd4[p1][:]).then_inc(d["inv"], 1)
                    dve.wait_ge(d["inv"], one + 1)
                    dve.tensor_tensor(rs4[p1][:], inv4[p1][:],
                                      weight[:, 0, bass.ds(one * G, G)],
                                      ALU.mult).then_inc(d["rs"], 1)
                    minus_mean_over_sd(nm4[p1], mv4[p1], rs4[p1], one, d["rs"], d["nm"])
                if in_range(i, B):
                    wait_apart(dve, d["moe"], i + 1)
                    stats(stats4[par], lambda j: moe[par][:, j, :], d["stats"])
                    mean_var(mv4[par], stats4[par], i, d["stats"], d["mv"])
                if in_range(i, B):
                    dve.wait_ge(d["mv"], i + 1)
                    dve.tensor_tensor(scaled_var[par][:], mv4[par][:, :, 1],
                                      weight0_square[:, bass.ds(i * G, G)],
                                      ALU.mult).then_inc(d["scaled"], 1)

            rounds_of_d(dve, d_round)

        @block.tensor
        def _(pe):
            pe.wait_ge(s_pool_const, 1)
            pe.wait_ge(s_small, 16 * 6)
            pe.transpose(p_hidden[:, 0:D], w_in[:], ident[:])
            pe.transpose(p_hidden[:, D:2 * D], w_out[:], ident[:]).then_inc(s_wT_ps, 1)

            def a_round(i, par):
                now, two, nxt = i, i - 2, i + 1
                if in_range(now, B):
                    if isinstance(now, int) and now == 0:
                        pe.wait_ge(s_wT, 1)
                    pe.wait_ge(a["mixed"], now + 1)
                    pe.matmul(p_hidden[:], w_inT[:], mixed, start=True,
                              stop=True).then_inc(a["hidden_ps"], 1)
                if in_range(two, B):
                    pe.wait_ge(a["xn2"], two + 1)
                    for j in range(G):
                        last = pe.transpose(p_xn2T[:, j * P:(j + 1) * P], row[par][:, j, 0:D],
                                            ident[:])
                    last.then_inc(a["xn2T_ps"], 1)
                    pe.wait_ge(a["xn2T"], two + 1)
                    for j in range(G):
                        last = pe.matmul(p_gate[:, j * E:(j + 1) * E],
                                         xn2T[:, j * P:(j + 1) * P], gate[:], start=True,
                                         stop=True)
                    last.then_inc(a["gate_ps"], 1)
                if in_range(nxt, B):
                    pe.wait_ge(a["xn1"], nxt + 1)
                    for j in range(G):
                        last = pe.transpose(p_xn1T[:, j * P:(j + 1) * P], xn1[:, j, :],
                                            ident[:])
                    last.then_inc(a["xn1T_ps"], 1)
                if in_range(now, B):
                    if isinstance(now, int) and now == 0:
                        pe.wait_ge(s_const, 8)
                    pe.wait_ge(a["states"], now + 1)
                    pe.matmul(p_attn[:], ones_b[0:BIAS_ROWS, :],
                              b_parts[:, None, :].broadcast_to([BIAS_ROWS, G, D]), start=True,
                              stop=False)
                    for j in range(G):
                        last = pe.matmul(p_attn[:, j * D:(j + 1) * D],
                                         states[:, j * P:(j + 1) * P], w_outT[:],
                                         start=False, stop=(j == G - 1))
                    last.then_inc(a["attn_ps"], 1)
                if in_range(two, B):
                    pe.wait_ge(a["total"], two + 1)
                    pe.matmul(p_rank[:, 0:G * E], before_b[:],
                              taken[par][:, 0:G, :].rearrange("p j e -> p (j e)"), start=True,
                              stop=False)
                    for j in range(G - 1):
                        pe.matmul(p_rank[:, (j + 1) * E:G * E], ones_b[:],
                                  taken[par][:, j:j + 1, :].broadcast_to([P, G - 1 - j, E]),
                                  start=False, stop=False)
                    pe.matmul(p_rank[:, 0:G * E], ones_b[:],
                              taken[par][:, G:G + 1, :].broadcast_to([P, G, E]), start=False,
                              stop=True).then_inc(a["rank_ps"], 1)

            rounds_of_a(pe, a_round)

            pe.wait_ge(a["place"], B)
            pe.matmul(p_rank[:, 0:E], ones_b[:], taken[B % 2][:, G, :], start=True,
                      stop=True).then_inc(s_count_ps, 1)

            pe.wait_ge(s_table, 1)

            def chunk_of(t):
                return pe.value_load(tile_chunk_i[0:1, bass.ds(t, 1)], min_val=0,
                                     max_val=(E - 1) * FC)

            def layer(to, x_hi, x_lo, first_chunk):
                w_hi, w_lo = (w_parts[:, bass.ds(first_chunk, FC), part, :] for part in (0, 1))
                pe.matmul(to, x_hi, w_hi, start=True, stop=False)
                pe.matmul(to, x_lo, w_hi, start=False, stop=False)
                return pe.matmul(to, x_hi, w_lo, start=False, stop=True)

            chunks = {}

            def c_round(base, r):
                t = base + r
                if in_range(t, TILES + 1):
                    wait(pe, c["x_lo"], t)
                if in_range(t, TILES):
                    pe.wait_ge(s_rows_in[r % UNROLL],
                               (16 // UNROLL) * base + 16 * (r // UNROLL + 1))
                    pe.transpose(p_xeT[:, 0:P], taken_rows[r % UNROLL][:, 0:D],
                                 ident[:]).then_inc(c["xeT_ps"], 1)
                t = base + (r - 1)
                if in_range(t, TILES):
                    if isinstance(t, int) and t == 0:
                        pe.wait_ge(s_w01_lo, 2)
                    if r == 0:
                        chunks[0] = chunk_of(t)
                    n = (r - 1) % 2
                    wait(pe, c["silu"], t)
                    layer(p_l1[:], x_hi[n][:], x_lo[n][:], chunks[r]).then_inc(c["l1_ps"], 1)
                    wait(pe, c["gated"], t)
                    layer(p_l2[:], x_hi[n][:], x_lo[n][:],
                          chunks[r] + W_CHUNKS).then_inc(c["l2_ps"], 1)
                if r + 1 < UNROLL and in_range(base + r, TILES):
                    chunks[r + 1] = chunk_of(base + r)
                if in_range(base + (r - 3), TILES):
                    chunk = chunks[r - 2] if r >= 2 else chunk_of(base + (r - 3))
                t = base + (r - 2)
                if in_range(t, TILES + 1):
                    wait(pe, c["g_lo"], t)
                if in_range(t, TILES):
                    if isinstance(t, int) and t == TILES - 1:
                        pe.wait_ge(c["gated"], TILES)
                    for n in range(FC):
                        last = pe.transpose(p_gatedT[:, n * P:(n + 1) * P],
                                            gated[r % 2][:, n * P:(n + 1) * P], ident[:])
                    last.then_inc(c["gatedT_ps"], 1)
                t = base + (r - 3)
                if in_range(t, TILES):
                    if isinstance(t, int) and t == 0:
                        pe.wait_ge(s_wo_lo, 1)
                    to = p_y[(r - 3) % 2]
                    for n in range(FC):
                        wo = w_parts[:, bass.ds(chunk + (2 * W_CHUNKS + n), 1), :, :]
                        of = slice(n * P, (n + 1) * P)
                        pe.matmul(to[:, 0:2 * D], g_hi[(r - 3) % 2][:, of],
                                  wo.rearrange("p o t d -> p (o t d)"), start=(n == 0),
                                  stop=False)
                        last = pe.matmul(to[:, 0:D], g_lo[(r - 3) % 2][:, of],
                                         wo[:, :, 0, :].rearrange("p o d -> p (o d)"),
                                         start=False, stop=(n == FC - 1))
                    last.then_inc(c["y_ps"], 1)

            rounds_of_tiles(pe, c_round)


_INS = ["L0_attn_x", "L0_attn_W_in", "L0_attn_b_in", "L0_attn_W_out", "L0_attn_b_out",
        "L0_attn_decay", "L0_attn_mix", "L0_ffn_gate_kernel", "L0_ffn_w0", "L0_ffn_w1",
        "L0_ffn_wo"]


def kernel(**inputs):
    import numpy as np
    import concourse.bacc as bacc
    from concourse import mybir as _mybir
    from concourse.bass_utils import run_bass_kernel_spmd

    nc = bacc.Bacc("TRN2", target_bir_lowering=False, num_devices=1)
    arrays, args = {}, []
    for name in _INS:
        array = np.ascontiguousarray(inputs[name]).reshape(np.shape(inputs[name]) or (1,))
        arrays["in_" + name] = array
        args.append(nc.dram_tensor("in_" + name, array.shape, _mybir.dt.from_np(array.dtype),
                                   kind="ExternalInput").ap())
    out = nc.dram_tensor("out_dram", (B, S, D), F32, kind="ExternalOutput").ap()
    sandwich_kernel(nc, *args, out)
    r = run_bass_kernel_spmd(nc, [arrays], core_ids=[0])
    return r.results[0]["out_dram"]
```

```python
from contextlib import ExitStack

import concourse.bass as bass
from concourse import mybir

F32 = mybir.dt.float32
F32R = mybir.dt.float32r
BF16 = mybir.dt.bfloat16
I32 = mybir.dt.int32
U32 = mybir.dt.uint32
ALU = mybir.AluOpType
ACT = mybir.ActivationFunctionType
AX = mybir.AxisListType

P = 128
B, S, D = 8, 512, 128
E, F, K = 8, 512, 2
T = B * S
G = S // P
FC = F // P
EPS = 1e-5
REGION = T + P
ROW = D + 2
UNROLL = 8
UNROLL_PE = 16
TILES = T * K // P + E - 1
LEAD = -TILES % UNROLL
LEAD_PE = -TILES % UNROLL_PE
SPARE = TILES - T * K // P
NO_PAIR = 2 * K * T
WCOLS = E * F
W_CHUNKS = WCOLS // D
BIAS_ROWS = 96
Y_SLOTS = 4


def sandwich_kernel(nc, x_in, w_in_in, b_in_in, w_out_in, b_out_in, decay_in, mix_in,
                    gate_in, w0_in, w1_in, wo_in, out):
    ctx = ExitStack()
    with ctx:
        def sb(name, shape, dt=F32):
            return ctx.enter_context(nc.sbuf_tensor("sb_" + name, shape, dt))

        def sem(name):
            return ctx.enter_context(nc.semaphore(name))

        def pair(name, shape, dt=F32):
            return [sb(f"{name}{n}", shape, dt) for n in range(2)]

        expert_rows = nc.dram_tensor("expert_rows", [E * REGION + SPARE * P, ROW], F32)
        pair_rows = nc.dram_tensor("pair_rows", [T * K, D], F32)

        x = sb("x", [P, B * G, D])
        w_raw = sb("w_raw", [P, 3 * WCOLS])
        w_raw_chunks = w_raw[:].rearrange("p (c d) -> p c d", d=D)
        w_parts = sb("w_parts", [P, 2 * W_CHUNKS, 2, D], F32R)
        w_in = sb("w_in", [P, D])
        w_out = sb("w_out", [P, D])
        w_inT = sb("w_inT", [P, D])
        w_outT = sb("w_outT", [P, D])
        gate = sb("gate", [P, E])
        b_in = sb("b_in", [P, 1])
        b_rows = sb("b_rows", [BIAS_ROWS, D])
        b_rest = sb("b_rest", [BIAS_ROWS, D])
        b_rest2 = sb("b_rest2", [BIAS_ROWS, D])
        b_part = [sb(f"b_part{n}", [BIAS_ROWS, D], BF16) for n in range(3)]
        b_parts = sb("b_parts", [BIAS_ROWS, D], BF16)
        decay = sb("decay", [P, 1])
        mix = sb("mix", [P, 1])
        one_minus_mix = sb("one_minus_mix", [P, 1])
        decay_row = sb("decay_row", [P, S])
        ident = sb("ident", [P, P])
        ones_f = sb("ones_f", [P, P])
        ones_b = sb("ones_b", [P, P], BF16)
        before_b = sb("before_b", [P, P], BF16)
        eps = sb("eps", [P, 1])
        unused = sb("unused", [P, 1])
        expert_i = sb("expert_i", [P, E], I32)
        expert_f = sb("expert_f", [P, E])
        region_f = sb("region_f", [P, E])
        token2_i = sb("token2_i", [P, B * G], I32)
        token2_f = sb("token2_f", [P, B * G])
        tile_i = sb("tile_i", [P, TILES], I32)
        tile_f = sb("tile_f", [P, TILES])
        pad_row = sb("pad_row", [P, ROW])

        stats1, stats2, stats3 = (pair(f"stats{n}_", [P, G, 6]) for n in (1, 2, 3))
        mv1, mv2, mv3 = (pair(f"mv{n}_", [P, G, 2]) for n in (1, 2, 3))
        sd1, sd2, sd3 = (pair(f"sd{n}_", [P, G]) for n in (1, 2, 3))
        rs1, rs2, rs3 = (pair(f"rs{n}_", [P, G]) for n in (1, 2, 3))
        nm1, nm2, nm3 = (pair(f"nm{n}_", [P, G]) for n in (1, 2, 3))
        early = sb("early", [P, 4 * S])
        mixed, hidden, xn1_flat, shifted = (early[:, n * S:(n + 1) * S] for n in range(4))
        xn1 = xn1_flat.rearrange("p (j d) -> p j d", j=G)
        states = sb("states", [P, S])
        normed2 = sb("normed2", [P, G, D])
        row = pair("row", [P, G, ROW])
        xn2T = sb("xn2T", [P, S])
        top8 = pair("top8_", [P, G, 8])
        choice8 = pair("choice8_", [P, G, 8], U32)
        choice_f = pair("choice_f", [P, K, G])
        onehot = pair("onehot", [P, K, G, E], BF16)
        taken = pair("taken", [P, G + 1, E], BF16)
        rank_f = pair("rank_f", [P, G, E])
        place4 = pair("place4_", [P, K, G, E])
        place = pair("place", [P, K, G], I32)
        logit_gap = sb("logit_gap", [P, B * G])
        weight = sb("weight", [P, K, B * G])
        denom = sb("denom", [P, B * G])
        weight0_square = sb("weight0_square", [P, B * G])

        count_i = sb("count_i", [P, E], I32)
        tiles_i = sb("tiles_i", [P, E], I32)
        tiles_f = sb("tiles_f", [P, E])
        ends = sb("ends", [P, E])
        skip = sb("skip", [P, E])
        past, past_skip = (early[:, n * TILES * E:(n + 1) * TILES * E].rearrange(
            "p (t e) -> p t e", t=TILES) for n in (0, 1))
        tile_expert = sb("tile_expert", [P, TILES])
        tile_chunk_i = sb("tile_chunk_i", [P, TILES], I32)
        tile_row = sb("tile_row", [P, TILES])
        tile_row_i = sb("tile_row_i", [P, TILES], I32)
        pad_start_i = sb("pad_start_i", [P, E], I32)

        taken_rows = [early[:, n * ROW:(n + 1) * ROW] for n in range(UNROLL)]
        y_rows = [early[:, UNROLL * ROW + n * D:UNROLL * ROW + (n + 1) * D]
                  for n in range(Y_SLOTS)]
        x_hi, x_lo = pair("x_hi", [P, P], F32R), pair("x_lo", [P, P], F32R)
        gatedT = pair("gatedT", [P, F])
        silu = [w_raw[:, n * F:(n + 1) * F] for n in (0, 1)]
        gated = [w_raw[:, n * F:(n + 1) * F] for n in (2, 3)]
        y_pair = [sb(f"y_pair{n}", [P, 1], I32) for n in range(Y_SLOTS)]

        pairs_in = w_raw[:, WCOLS:WCOLS + B * G * K * D].rearrange(
            "p (b j k d) -> p b j k d", b=B, j=G, k=K)
        normed4 = [w_raw[:, n * G * D:(n + 1) * G * D].rearrange(
            "p (j d) -> p j d", j=G) for n in (4, 5)]
        scaled_var = pair("scaled_var", [P, G])
        inv4 = pair("inv4_", [P, G])
        stats4, mv4 = pair("stats4_", [P, G, 6]), pair("mv4_", [P, G, 2])
        sd4, rs4, nm4 = pair("sd4_", [P, G]), pair("rs4_", [P, G]), pair("nm4_", [P, G])

        bank = [ctx.enter_context(nc.psum_tensor(f"bank{n}", [P, 512], F32)) for n in range(8)]
        p_xn1T, p_hidden, p_xn2T, p_gate, p_rank = bank[:5]
        p_attn = bank[5:7]
        p_xeT, p_l1, p_l2, p_gatedT = bank[:4]
        p_y = bank[4:6]

        s_x = [sem("x_batch0_in"), sem("x_batch1_in"), sem("x_batch2_in"), sem("x_rest_in")]
        s_small, s_bias_in = sem("small_in"), sem("bias_in")
        s_w_in = [sem("w0_in"), sem("w1_in"), sem("wo_in")]
        s_w_hi = [sem("w0_hi"), sem("w1_hi")]
        s_w_lo = [sem("w0_lo"), sem("w1_lo")]
        s_pool_const, s_pool_step, s_const = sem("pool_const"), sem("pool_step"), sem("const")
        s_wT_ps, s_wT = sem("wT_ps"), sem("wT")
        s_apart = sem("waited_apart")
        names_a = ("stats1 mv1 sd1 rs1 xn1 xn1T_ps shifted mixed hidden_ps hidden states attn_ps "
                   "nm1 nm3 stats2 mv2 sd2 rs2 nm2 normed2 x1 stats3 mv3 sd3 rs3 xn2 "
                   "xn2T_ps xn2T gate_ps gap top8 choice choice_f onehot taken total "
                   "rank_ps rank place4 place")
        a = {n: sem("a_" + n) for n in names_a.split()}
        s_sent = [sem("rows_sent_even"), sem("rows_sent_odd")]
        s_count_ps, s_b, s_table, s_pads = sem("count_ps"), sem("b_step"), sem("table"), sem("pads")
        s_exp = sem("exp")
        names_c = "xeT_ps x_hi x_lo l1_ps l2_ps silu gated gatedT_ps gatedT y_ps y"
        c = {n: sem("c_" + n) for n in names_c.split()}
        s_rows_in = [sem(f"tile_in{n}") for n in range(UNROLL)]
        s_y_sent = [sem(f"y_sent{n}") for n in range(Y_SLOTS)]
        names_d = "weighed m stats mv scaled sd inv rs nm normed out"
        d = {n: sem("d_" + n) for n in names_d.split()}
        s_pairs_in = [sem("pairs_in_even"), sem("pairs_in_odd")]
        s_out = sem("out_written")

        def wait(eng, s, value):
            if not (isinstance(value, int) and value <= 0):
                eng.wait_ge(s, value)

        def wait_apart(eng, s, value):
            eng.wait_ge(s, value).then_inc(s_apart, 1)

        def in_range(n, count):
            return not isinstance(n, int) or 0 <= n < count

        def steps_of(*steps):
            for step, b, n in steps:
                if in_range(b, B):
                    step(b, n)

        def rounds_of_a(eng, a_round):
            for i in (-2, -1, 0, 1):
                a_round(i, i % 2)
            with eng.Fori(2, B - 3, 2) as i:
                for r in (0, 1):
                    a_round(i + r, r)
            for i in range(B - 2, B + 2):
                a_round(i, i % 2)

        def rounds_of_d(eng, a_round):
            for i in (0, 1, 2):
                a_round(i, i % 2)
            with eng.Fori(3, B - 2, 2) as i:
                for r in (0, 1):
                    a_round(i + r, 1 - r)
            for i in (B - 1, B):
                a_round(i, i % 2)

        def rounds_of_tiles(eng, a_round, unroll=UNROLL, lead=LEAD):
            for r in range(unroll - lead):
                a_round(0, r)
            with eng.Fori(unroll, TILES + lead - unroll + 1, unroll) as base:
                for r in range(-lead, unroll - lead):
                    a_round(base, r)
            for r in range(-lead, 3 - lead):
                a_round(TILES + lead, r)

        def chunks_of(n):
            return slice(n * W_CHUNKS, (n + 1) * W_CHUNKS)

        def subtract_hi(eng, n):
            return eng.tensor_tensor(w_parts[:, chunks_of(n), 1, :], w_raw_chunks[:, chunks_of(n)],
                                     w_parts[:, chunks_of(n), 0, :].bitcast(F32), ALU.subtract)

        def x_tile(b):
            return lambda j: x[:, bass.ds(b * G + j, 1), :].rearrange("p o d -> p (o d)")

        def y_of(b, k):
            return pairs_in[:, bass.ds(b, 1), :, k, :].rearrange("p o j d -> p (o j) d")

        def m_tile(b):
            return lambda j: pairs_in[:, bass.ds(b, 1), j, 0, :].rearrange("p o d -> p (o d)")

        def tiles_of(t, b):
            return t[:, bass.ds(b * G, G)]

        def pad_experts(eng, first_expert):
            eng.wait_ge(s_b, 2)
            for e in range(first_expert, E, 2):
                first = eng.value_load(pad_start_i[0:1, e:e + 1], min_val=e * REGION,
                                       max_val=e * REGION + T)
                eng.dma_start(expert_rows[bass.ds(first, P), :], pad_row[:]).then_inc(s_pads, 16)

        block = ctx.enter_context(nc.Block())

        @block.sync
        def _(sp):
            tokens = x_in.rearrange("b (j p) d -> p (b j) d", p=P)
            sp.dma_start(x[:, 0:G], tokens[:, 0:G]).then_inc(s_x[0], 16)
            sp.dma_start(gate[:], gate_in).then_inc(s_small, 16)
            sp.dma_start(b_rows[:], b_out_in.rearrange("(o n) -> o n", o=1).broadcast_to(
                [BIAS_ROWS, D])).then_inc(s_bias_in, 16)
            sp.dma_start(x[:, G:2 * G], tokens[:, G:2 * G]).then_inc(s_x[1], 16)
            sp.wait_ge(s_small, 16 * 6)
            sp.dma_start(x[:, 2 * G:3 * G], tokens[:, 2 * G:3 * G]).then_inc(s_x[2], 16)
            sp.dma_start(x[:, 3 * G:], tokens[:, 3 * G:]).then_inc(s_x[3], 16)
            for n, w in enumerate((w0_in, w1_in)):
                sp.dma_start(w_raw[:, n * WCOLS:(n + 1) * WCOLS].rearrange(
                    "p (e f) -> p e f", e=E), w.rearrange("e d f -> d e f")
                             ).then_inc(s_w_in[n], 16)
            sp.dma_start(w_raw[:, 2 * WCOLS:].rearrange("p (e c n) -> p e c n", e=E, c=FC),
                         wo_in.rearrange("e (c p) n -> p e c n", p=P)).then_inc(s_w_in[2], 16)

            pad_experts(sp, 0)
            sp.wait_ge(s_table, 1)

            def first_row(t):
                return sp.value_load(tile_row_i[0:1, bass.ds(t, 1)], min_val=0,
                                     max_val=E * REGION + (SPARE - 1) * P)

            def load_tile(first, r):
                sp.dma_start(taken_rows[r][:],
                             expert_rows[bass.ds(first, P), :]).then_inc(s_rows_in[r], 16)

            ahead = [first_row(r) for r in range(4)]
            sp.wait_ge(s_pads, 16 * E)
            sp.wait_ge(s_sent[0], 16 * K * G * (B // 2))
            sp.wait_ge(s_sent[1], 16 * K * G * (B // 2) + 16 * SPARE)
            for r in range(UNROLL):
                load_tile(ahead[r] if r < len(ahead) else first_row(r), r)
            for r in range(UNROLL - LEAD):
                sp.wait_ge(c["y"], r + 1)
                load_tile(first_row(UNROLL + r), r)
            with sp.Fori(2 * UNROLL, TILES + LEAD - UNROLL + 1, UNROLL) as base:
                for r in range(-LEAD, UNROLL - LEAD):
                    sp.wait_ge(c["y"], base + (r - UNROLL + 1))
                    load_tile(first_row(base + r), r % UNROLL)

            for n in range(Y_SLOTS):
                sp.wait_ge(s_y_sent[n], 16 * len(range(n, TILES, Y_SLOTS)))
            pairs = pair_rows[:].rearrange("(b j p k) d -> b p j k d", b=B, p=P, k=K)

            def load_pairs(b, par):
                sp.dma_start(pairs_in[:, bass.ds(b, 1)].rearrange("p o j k d -> p (o j k d)"),
                             pairs[bass.ds(b, 1)].rearrange("o p j k d -> (o p) j k d")
                             ).then_inc(s_pairs_in[par], 16)

            for b in (0, 1):
                load_pairs(b, b)
            with sp.Fori(2, B - 1, 2) as b:
                for r in (0, 1):
                    sp.wait_ge(s_pairs_in[r], 8 * b)
                    load_pairs(b + r, r)
            results = out.rearrange("b (j p) d -> b p j d", p=P)
            with sp.Fori(0, B) as b:
                sp.wait_ge(d["out"], b + 1)
                sp.dma_start(results[bass.ds(b, 1)].rearrange("o p j d -> (o p) j d"),
                             tiles_of(x, b)).then_inc(s_out, 16)
            sp.wait_ge(s_out, 16 * B)

        @block.gpsimd
        def _(pool):
            pool.memset(ident[:], 0.0)
            pool.memset(before_b[:], 1.0)
            pool.memset(ones_f[:], 1.0)
            pool.memset(ones_b[:], 1.0)
            pool.memset(pad_row[:], 0.0).then_inc(s_pool_step, 1)
            pool.wait_ge(s_pool_step, 1)
            pool.affine_select(out=ident[:], in_=ident[:], compare_op=ALU.not_equal, fill=1.0,
                               base=0, pattern=[[-1, P]], channel_multiplier=1)
            pool.affine_select(out=before_b[:], in_=before_b[:], compare_op=ALU.is_gt, fill=0.0,
                               base=0, pattern=[[1, P]], channel_multiplier=-1)
            pool.memset(pad_row[:, D:D + 1], float(NO_PAIR))
            pool.iota(expert_i[:], pattern=[[1, E]], base=0, channel_multiplier=0)
            pool.iota(token2_i[:], pattern=[[2 * P, B * G]], base=0, channel_multiplier=2)
            pool.iota(tile_i[:], pattern=[[1, TILES]], base=0,
                      channel_multiplier=0).then_inc(s_pool_const, 1)
            pool.wait_ge(s_pool_const, 1)
            for n in range(SPARE):
                first = E * REGION + n * P
                pool.dma_start(expert_rows[first:first + P, :], pad_row[:]).then_inc(s_sent[1], 16)

            pool.wait_ge(s_w_hi[0], 1)
            subtract_hi(pool, 0).then_inc(s_w_lo[0], 1)

            def a_round(i, par):
                b = i - 2
                if in_range(b, B):
                    wait_apart(pool, a["place"], b + 1)
                    for j in range(G):
                        for k in range(K):
                            pool.indirect_dma_start(
                                expert_rows[:, :],
                                bass.IndirectOffsetOnAxis(ap=place[par][:, k, j:j + 1], axis=0),
                                row[par][:, j, :], None).then_inc(s_sent[par], 16)

            rounds_of_a(pool, a_round)

            def c_round(base, r):
                t = base + (r - 3)
                if in_range(t, TILES):
                    slot = (r - 3) % Y_SLOTS
                    wait_apart(pool, c["y"], t + 1)
                    pool.indirect_dma_start(
                        pair_rows[:, :],
                        bass.IndirectOffsetOnAxis(ap=y_pair[slot][:, 0:1], axis=0),
                        y_rows[slot][:], None, bounds_check=T * K - 1,
                        oob_is_err=False).then_inc(s_y_sent[slot], 16)

            rounds_of_tiles(pool, c_round)

            pool.wait_ge(s_exp, 1)

            def weigh(b, par):
                pool.wait_ge(s_pairs_in[par], 8 * (b - par) + 16)
                rows = y_of(b, 1)
                pool.tensor_tensor(rows, rows, weight[:, 1, bass.ds(b * G, G), None].broadcast_to(
                    [P, G, D]), ALU.mult).then_inc(d["weighed"], 1)

            def add(b, par):
                pool.wait_ge(d["normed"], b + 1)
                pool.tensor_tensor(tiles_of(x, b), tiles_of(x, b), normed4[par],
                                   ALU.add).then_inc(d["out"], 1)

            for b in range(4):
                weigh(b, b % 2)
            with pool.Fori(0, B - 5, 2) as b:
                for r in (0, 1):
                    add(b + r, r)
                    weigh(b + (r + 4), r)
            for b in range(B - 4, B):
                add(b, b % 2)

        @block.scalar
        def _(act):
            for to, of in ((decay, decay_in), (mix, mix_in)):
                act.dma_start(to[:], of.rearrange("(o n) -> o n", o=1).broadcast_to(
                    [P, 1])).then_inc(s_small, 16)
            act.dma_start(w_in[:], w_in_in).then_inc(s_small, 16)
            act.dma_start(w_out[:], w_out_in).then_inc(s_small, 16)
            act.dma_start(b_in[:], b_in_in.rearrange("(p o) -> p o", o=1)).then_inc(s_small, 16)
            act.wait_ge(s_const, 1)

            def root(to, of, name_in, name_out):
                def step(b, n):
                    act.wait_ge(a[name_in], b + 1)
                    act.activation(to[n][:], of[n][:, :, 1], ACT.Sqrt,
                                   bias=eps[:]).then_inc(a[name_out], 1)
                return step

            def normalise(to, of, rs, nm, s_done):
                for j in range(G):
                    last = act.activation(to(j), of(j), ACT.Identity, scale=rs[:, j:j + 1],
                                          bias=nm[:, j:j + 1])
                last.then_inc(s_done, 1)

            root1, root2, root3 = (root(*of) for of in (
                (sd1, mv1, "mv1", "sd1"), (sd2, mv2, "mv2", "sd2"), (sd3, mv3, "mv3", "sd3")))

            def normalise1(b, n):
                act.wait_ge(a["nm1"], b + 1)
                normalise(lambda j: xn1[:, j, :], x_tile(b), rs1[n], nm1[n], a["xn1"])

            def shift(b, n):
                if isinstance(b, int) and b == 0:
                    act.wait_ge(s_const, 2)
                act.wait_ge(a["xn1T_ps"], b + 1)
                act.activation(shifted[:, 1:S], p_xn1T[:, 0:S - 1], ACT.Copy,
                               scale=one_minus_mix[:]).then_inc(a["shifted"], 1)

            def relu(b, n):
                act.wait_ge(a["hidden_ps"], b + 1)
                act.activation(hidden, p_hidden[:], ACT.Relu,
                               bias=b_in[:]).then_inc(a["hidden"], 1)

            def normalise2(b, n):
                act.wait_ge(a["nm2"], b + 1)
                normalise(lambda j: normed2[:, j, :], lambda j: p_attn[n][:, j * D:(j + 1) * D],
                          rs2[n], nm2[n], a["normed2"])

            def normalise3(b, n):
                if n:
                    wait(act, s_sent[1], 8 * K * G * (b - 1) + 16 * SPARE)
                else:
                    wait(act, s_sent[0], 8 * K * G * b)
                act.wait_ge(a["nm3"], b + 1)
                normalise(lambda j: row[n][:, j, 0:D], x_tile(b), rs3[n], nm3[n], a["xn2"])

            def turned(b, n):
                act.wait_ge(a["xn2T_ps"], b + 1)
                act.activation(xn2T[:], p_xn2T[:], ACT.Copy).then_inc(a["xn2T"], 1)

            def a_round(i, par):
                now, one, two, nxt = i, i - 1, i - 2, i + 1
                odd = 1 - par
                steps_of((turned, two, par), (root2, one, odd), (normalise2, one, odd),
                         (normalise1, nxt, odd), (relu, now, par), (root1, i + 2, par),
                         (root3, one, odd), (shift, nxt, odd), (normalise3, one, odd))

            rounds_of_a(act, a_round)
            act.wait_ge(s_w_in[1], 16)
            act.activation(w_parts[:, chunks_of(1), 0, :], w_raw_chunks[:, chunks_of(1)],
                           ACT.Copy).then_inc(s_w_hi[1], 1)
            pad_experts(act, 1)
            act.activation(unused[:], eps[:], ACT.Silu)

            def c_round(base, r):
                t = base + r
                if in_range(t, TILES):
                    act.wait_ge(c["xeT_ps"], t + 1)
                    act.activation(x_hi[r % 2][:], p_xeT[:, 0:P], ACT.Copy).then_inc(c["x_hi"], 1)
                t = base + (r - 1)
                if in_range(t, TILES):
                    act.wait_ge(c["l1_ps"], t + 1)
                    act.activation(silu[(r - 1) % 2][:], p_l1[:],
                                   ACT.Silu).then_inc(c["silu"], 1)
                t = base + (r - 2)
                if in_range(t, TILES):
                    act.wait_ge(c["gatedT_ps"], t + 1)
                    act.activation(gatedT[r % 2][:], p_gatedT[:],
                                   ACT.Copy).then_inc(c["gatedT"], 1)

            rounds_of_tiles(act, c_round)

            act.wait_ge(a["gap"], B)
            act.activation(weight[:, 1, :], logit_gap[:], ACT.Exp).then_inc(s_exp, 1)

            def d_round(i, par):
                if in_range(i, B):
                    act.wait_ge(d["scaled"], i + 1)
                    act.activation(sd4[par][:], scaled_var[par][:], ACT.Sqrt,
                                   bias=eps[:]).then_inc(d["sd"], 1)
                b = i - 1
                if in_range(b, B):
                    wait(act, d["out"], b - 1)
                    act.wait_ge(d["nm"], b + 1)
                    normalise(lambda j: normed4[1 - par][:, j, :],
                              m_tile(b), rs4[1 - par], nm4[1 - par], d["normed"])

            rounds_of_d(act, d_round)

        @block.vector
        def _(dve):
            dve.memset(eps[:], EPS)
            dve.memset(shifted[:, 0:1], 0.0)
            dve.memset(b_parts[:], 0.0)
            dve.memset(taken[0][:, G, :], 0.0).then_inc(s_const, 1)

            def constants():
                dve.wait_ge(s_pool_const, 1)
                dve.tensor_copy(expert_f[:], expert_i[:])
                dve.tensor_scalar(region_f[:], expert_i[:], float(REGION), None, ALU.mult)
                dve.tensor_copy(token2_f[:], token2_i[:])
                dve.tensor_copy(tile_f[:], tile_i[:])
                dve.wait_ge(s_small, 16 * 6)
                dve.tensor_scalar(one_minus_mix[:], mix[:], -1.0, 1.0, ALU.mult,
                                  ALU.add).then_inc(s_const, 1)
                dve.tensor_scalar(decay_row[:].rearrange("p (j n) -> p j n", j=G),
                                  ones_f[:, None, :].broadcast_to([P, G, P]), decay[:], None,
                                  ALU.mult)
                dve.wait_ge(s_wT_ps, 1)
                dve.tensor_copy(w_inT[:], p_hidden[:, 0:D])
                dve.tensor_copy(w_outT[:], p_hidden[:, D:2 * D]).then_inc(s_wT, 1)

            def split_bias():
                dve.wait_ge(s_bias_in, 16)
                dve.tensor_copy(b_part[0][:], b_rows[:]).then_inc(s_const, 1)
                dve.wait_ge(s_const, 3)
                dve.tensor_tensor(b_rest[:], b_rows[:], b_part[0][:],
                                  ALU.subtract).then_inc(s_const, 1)
                dve.wait_ge(s_const, 4)
                dve.tensor_copy(b_part[1][:], b_rest[:]).then_inc(s_const, 1)
                dve.wait_ge(s_const, 5)
                dve.tensor_tensor(b_rest2[:], b_rest[:], b_part[1][:],
                                  ALU.subtract).then_inc(s_const, 1)
                dve.wait_ge(s_const, 6)
                dve.tensor_copy(b_part[2][:], b_rest2[:]).then_inc(s_const, 1)
                dve.wait_ge(s_const, 7)
                for n in range(3):
                    last = dve.tensor_copy(b_parts[32 * n:32 * n + 1, :],
                                           b_part[n][32 * n:32 * n + 1, :])
                last.then_inc(s_const, 1)

            def stats(to, rows, s_stats):
                for j in range(G):
                    last = dve.bn_stats(to[:, j, :], rows(j))
                last.then_inc(s_stats, 1)

            def mean_var(mv, of, b, s_stats, s_mv):
                wait_apart(dve, s_stats, b + 1)
                for j in range(G):
                    last = dve.bn_aggr(mv[:, j, :], of[:, j, :])
                last.then_inc(s_mv, 1)

            def minus_mean_over_sd(nm, mv, rs, b, s_rs, s_nm):
                dve.wait_ge(s_rs, b + 1)
                dve.scalar_tensor_tensor(out=nm[:], in0=mv[:, :, 0], scalar=-1.0, in1=rs[:],
                                         op0=ALU.mult, op1=ALU.mult).then_inc(s_nm, 1)

            norms = {1: (stats1, mv1, sd1, rs1, nm1), 2: (stats2, mv2, sd2, rs2, nm2),
                     3: (stats3, mv3, sd3, rs3, nm3)}

            def mv_step(k):
                def step(b, n):
                    mean_var(norms[k][1][n], norms[k][0][n], b, a[f"stats{k}"], a[f"mv{k}"])
                return step

            def rs_step(k):
                def step(b, n):
                    dve.wait_ge(a[f"sd{k}"], b + 1)
                    dve.reciprocal(norms[k][3][n][:], norms[k][2][n][:]).then_inc(a[f"rs{k}"], 1)
                return step

            def nm_step(k):
                def step(b, n):
                    minus_mean_over_sd(norms[k][4][n], norms[k][1][n], norms[k][3][n], b,
                                       a[f"rs{k}"], a[f"nm{k}"])
                return step

            means1, means2, means3 = (mv_step(k) for k in (1, 2, 3))
            inverse1, inverse2, inverse3 = (rs_step(k) for k in (1, 2, 3))
            offset1, offset2, offset3 = (nm_step(k) for k in (1, 2, 3))

            def sums1(b, n):
                if isinstance(b, int) and b < len(s_x):
                    dve.wait_ge(s_x[b], 16)
                stats(stats1[n], x_tile(b), a["stats1"])

            def sums2(b, n):
                wait_apart(dve, a["attn_ps"], b + 1)
                stats(stats2[n], lambda j: p_attn[n][:, j * D:(j + 1) * D], a["stats2"])

            def sums3(b, n):
                wait_apart(dve, a["x1"], b + 1)
                stats(stats3[n], x_tile(b), a["stats3"])

            def mix_rows(b, n):
                dve.wait_ge(a["shifted"], b + 1)
                dve.scalar_tensor_tensor(out=mixed, in0=p_xn1T[:], scalar=mix[:], in1=shifted,
                                         op0=ALU.mult, op1=ALU.add).then_inc(a["mixed"], 1)

            def scan(b, n):
                if isinstance(b, int) and b == 0:
                    split_bias()
                dve.wait_ge(a["hidden"], b + 1)
                dve.tensor_tensor_scan(states[:], decay_row[:], hidden, 0.0, ALU.mult,
                                       ALU.add).then_inc(a["states"], 1)

            def residual(b, n):
                dve.wait_ge(a["normed2"], b + 1)
                dve.tensor_tensor(tiles_of(x, b), tiles_of(x, b), normed2[:],
                                  ALU.add).then_inc(a["x1"], 1)

            logits = p_gate[:, 0:G * E].rearrange("p (j e) -> p j e", j=G)

            def top(b, n):
                wait_apart(dve, a["gate_ps"], b + 1)
                for j in range(G):
                    last = dve.max(top8[n][:, j, :], logits[:, j, :])
                last.then_inc(a["top8"], 1)

            def top_experts(b, n):
                wait_apart(dve, a["top8"], b + 1)
                for j in range(G):
                    last = dve.max_index(choice8[n][:, j, :], top8[n][:, j, :], logits[:, j, :])
                last.then_inc(a["choice"], 1)
                dve.tensor_tensor(logit_gap[:, bass.ds(b * G, G)], top8[n][:, :, 1],
                                  top8[n][:, :, 0], ALU.subtract).then_inc(a["gap"], 1)

            def choices(b, n):
                dve.wait_ge(a["choice"], b + 1)
                dve.tensor_copy(choice_f[n][:], choice8[n][:, :, 0:K].rearrange(
                    "p j k -> p k j")).then_inc(a["choice_f"], 1)

            def one_hot(b, n):
                dve.wait_ge(a["choice_f"], b + 1)
                dve.tensor_tensor(
                    onehot[n][:].rearrange("p k j e -> p (k j) e"),
                    expert_f[:, None, :].broadcast_to([P, K * G, E]),
                    choice_f[n][:].rearrange("p k j -> p (k j)")[:, :, None].broadcast_to(
                        [P, K * G, E]), ALU.is_equal).then_inc(a["onehot"], 1)
                dve.tensor_copy(row[n][:, :, D + 1], choice_f[n][:, 0, :])
                dve.tensor_copy(row[n][:, :, D], token2_f[:, bass.ds(b * G, G)])

            def taken_by(b, n):
                dve.wait_ge(a["onehot"], b + 1)
                dve.tensor_tensor(taken[n][:, 0:G, :], onehot[n][:, 0], onehot[n][:, 1],
                                  ALU.add).then_inc(a["taken"], 1)

            def taken_so_far(b, n):
                dve.wait_ge(a["taken"], b + 1)
                with nc.allow_low_precision("whole numbers up to 32"):
                    dve.tensor_reduce(taken[1 - n][:, G, :],
                                      taken[n][:].rearrange("p j e -> p e j"), axis=AX.X,
                                      op=ALU.add).then_inc(a["total"], 1)

            def rank(b, n):
                dve.wait_ge(a["rank_ps"], b + 1)
                dve.tensor_tensor(rank_f[n][:],
                                  p_rank[:, 0:G * E].rearrange("p (j e) -> p j e", j=G),
                                  region_f[:, None, :].broadcast_to([P, G, E]),
                                  ALU.add).then_inc(a["rank"], 1)

            def chosen_rank(b, n):
                dve.wait_ge(a["rank"], b + 1)
                for k in range(K):
                    last = dve.tensor_tensor(place4[n][:, k], onehot[n][:, k], rank_f[n][:],
                                             ALU.mult)
                last.then_inc(a["place4"], 1)

            def places(b, n):
                dve.wait_ge(a["place4"], b + 1)
                with nc.allow_low_precision("whole numbers below 2 ** 24"):
                    dve.tensor_reduce(place[n][:], place4[n][:], axis=AX.X,
                                      op=ALU.add).then_inc(a["place"], 1)

            def a_round(i, par):
                now, one, two, nx2 = i, i - 1, i - 2, i + 2
                odd = 1 - par
                steps_of((mix_rows, now, par), (sums2, one, odd), (means2, one, odd),
                         (inverse2, one, odd), (offset2, one, odd), (sums1, nx2, par),
                         (top, two, par), (means1, nx2, par), (top_experts, two, par),
                         (choices, two, par), (residual, one, odd), (one_hot, two, par),
                         (taken_by, two, par), (sums3, one, odd), (taken_so_far, two, par),
                         (scan, now, par), (inverse1, nx2, par), (means3, one, odd),
                         (rank, two, par), (inverse3, one, odd), (offset1, nx2, par))
                if isinstance(i, int) and i == -2:
                    constants()
                steps_of((offset3, one, odd), (chosen_rank, two, par), (places, two, par))
                if isinstance(i, int) and i == 1:
                    dve.wait_ge(s_w_in[0], 16)
                    dve.tensor_copy(w_parts[:, chunks_of(0), 0, :],
                                    w_raw_chunks[:, chunks_of(0)]).then_inc(s_w_hi[0], 1)

            rounds_of_a(dve, a_round)

            steps = [0]

            def step(ins):
                steps[0] += 1
                ins.then_inc(s_b, 1)
                dve.wait_ge(s_b, steps[0])

            dve.wait_ge(s_count_ps, 1)
            dve.tensor_tensor(pad_start_i[:], p_rank[:, 0:E], region_f[:], ALU.add)
            step(dve.tensor_scalar(count_i[:], p_rank[:, 0:E], float(P - 1), None, ALU.add))
            step(dve.tensor_scalar(tiles_i[:], count_i[:], P.bit_length() - 1, None,
                                   ALU.arith_shift_right))
            step(dve.tensor_copy(tiles_f[:], tiles_i[:]))
            step(dve.tensor_tensor_scan(ends[:], ones_f[:, 0:E], tiles_f[:], 0.0, ALU.mult,
                                        ALU.add))
            dve.tensor_scalar(skip[:], tiles_f[:], -float(P), float(REGION), ALU.mult, ALU.add)
            step(dve.tensor_tensor(past[:], tile_f[:, :, None].broadcast_to([P, TILES, E]),
                                   ends[:, None, :].broadcast_to([P, TILES, E]), ALU.is_ge))
            dve.tensor_reduce(tile_expert[:], past[:], axis=AX.X, op=ALU.add)
            step(dve.tensor_tensor(past_skip[:], past[:],
                                   skip[:, None, :].broadcast_to([P, TILES, E]), ALU.mult))
            step(dve.tensor_reduce(tile_row[:], past_skip[:], axis=AX.X, op=ALU.add))
            dve.tensor_scalar(tile_chunk_i[:], tile_expert[:], float(E - 1), float(FC), ALU.min,
                              ALU.mult)
            dve.scalar_tensor_tensor(out=tile_row_i[:], in0=tile_f[:], scalar=float(P),
                                     in1=tile_row[:], op0=ALU.mult,
                                     op1=ALU.add).then_inc(s_table, 1)
            dve.wait_ge(s_w_hi[1], 1)
            subtract_hi(dve, 1).then_inc(s_w_lo[1], 1)

            def c_round(base, r):
                t = base + r
                if in_range(t, TILES):
                    dve.wait_ge(c["x_hi"], t + 1)
                    dve.tensor_tensor(x_lo[r % 2][:], p_xeT[:, 0:P], x_hi[r % 2][:].bitcast(F32),
                                      ALU.subtract).then_inc(c["x_lo"], 1)
                t = base + (r - 1)
                if in_range(t, TILES):
                    dve.wait_ge(c["silu"], t + 1)
                    dve.wait_ge(c["l2_ps"], t + 1)
                    dve.tensor_tensor(gated[(r - 1) % 2][:], p_l2[:], silu[(r - 1) % 2][:],
                                      ALU.mult).then_inc(c["gated"], 1)
                t = base + (r - 3)
                if in_range(t, TILES):
                    slot = (r - 3) % Y_SLOTS
                    dve.wait_ge(c["y_ps"], t + 1)
                    wait(dve, s_y_sent[slot],
                         (16 // Y_SLOTS) * base + 16 * ((r - 3) // Y_SLOTS))
                    source = taken_rows[(r - 3) % UNROLL]
                    dve.scalar_tensor_tensor(
                        out=y_pair[slot][:], in0=source[:, D + 1:D + 2],
                        scalar=tile_expert[:, bass.ds(t, 1)], in1=source[:, D:D + 1],
                        op0=ALU.not_equal, op1=ALU.add)
                    dve.tensor_copy(y_rows[slot][:], p_y[(r - 3) % 2][:, 0:D]
                                    ).then_inc(c["y"], 1)

            rounds_of_tiles(dve, c_round)

            dve.wait_ge(s_exp, 1)
            step(dve.tensor_scalar(denom[:], weight[:, 1, :], 1.0, None, ALU.add))
            step(dve.reciprocal(weight[:, 0, :], denom[:]))
            step(dve.tensor_tensor(weight0_square[:], weight[:, 0, :], weight[:, 0, :], ALU.mult))

            def d_round(i, par):
                one, p1 = i - 1, 1 - par
                if in_range(i, B):
                    dve.wait_ge(d["weighed"], i + 1)
                    dve.tensor_tensor(y_of(i, 0), y_of(i, 0), y_of(i, 1),
                                      ALU.add).then_inc(d["m"], 1)
                if in_range(one, B):
                    dve.wait_ge(d["sd"], one + 1)
                    dve.reciprocal(inv4[p1][:], sd4[p1][:]).then_inc(d["inv"], 1)
                if in_range(i, B):
                    wait_apart(dve, d["m"], i + 1)
                    stats(stats4[par], m_tile(i), d["stats"])
                if in_range(one, B):
                    dve.wait_ge(d["inv"], one + 1)
                    dve.tensor_tensor(rs4[p1][:], inv4[p1][:], weight[:, 0, bass.ds(one * G, G)],
                                      ALU.mult).then_inc(d["rs"], 1)
                if in_range(i, B):
                    mean_var(mv4[par], stats4[par], i, d["stats"], d["mv"])
                if in_range(one, B):
                    minus_mean_over_sd(nm4[p1], mv4[p1], rs4[p1], one, d["rs"], d["nm"])
                if in_range(i, B):
                    dve.wait_ge(d["mv"], i + 1)
                    dve.tensor_tensor(scaled_var[par][:], mv4[par][:, :, 1],
                                      weight0_square[:, bass.ds(i * G, G)],
                                      ALU.mult).then_inc(d["scaled"], 1)

            rounds_of_d(dve, d_round)

        @block.tensor
        def _(pe):
            pe.wait_ge(s_pool_const, 1)
            pe.wait_ge(s_small, 16 * 6)
            pe.transpose(p_hidden[:, 0:D], w_in[:], ident[:])
            pe.transpose(p_hidden[:, D:2 * D], w_out[:], ident[:]).then_inc(s_wT_ps, 1)

            def turn1(b, n):
                pe.wait_ge(a["xn1"], b + 1)
                for j in range(G):
                    last = pe.transpose(p_xn1T[:, j * P:(j + 1) * P], xn1[:, j, :], ident[:])
                last.then_inc(a["xn1T_ps"], 1)

            def times_w_in(b, n):
                if isinstance(b, int) and b == 0:
                    pe.wait_ge(s_wT, 1)
                pe.wait_ge(a["mixed"], b + 1)
                pe.matmul(p_hidden[:], w_inT[:], mixed, start=True,
                          stop=True).then_inc(a["hidden_ps"], 1)

            def times_w_out(b, n):
                if isinstance(b, int) and b == 0:
                    pe.wait_ge(s_const, 8)
                pe.wait_ge(a["states"], b + 1)
                pe.matmul(p_attn[n][:], ones_b[0:BIAS_ROWS, :],
                          b_parts[:, None, :].broadcast_to([BIAS_ROWS, G, D]), start=True,
                          stop=False)
                for j in range(G):
                    last = pe.matmul(p_attn[n][:, j * D:(j + 1) * D],
                                     states[:, j * P:(j + 1) * P], w_outT[:], start=False,
                                     stop=(j == G - 1))
                last.then_inc(a["attn_ps"], 1)

            def turn2(b, n):
                pe.wait_ge(a["xn2"], b + 1)
                for j in range(G):
                    last = pe.transpose(p_xn2T[:, j * P:(j + 1) * P], row[n][:, j, 0:D], ident[:])
                last.then_inc(a["xn2T_ps"], 1)

            def times_gate(b, n):
                pe.wait_ge(a["xn2T"], b + 1)
                for j in range(G):
                    last = pe.matmul(p_gate[:, j * E:(j + 1) * E], xn2T[:, j * P:(j + 1) * P],
                                     gate[:], start=True, stop=True)
                last.then_inc(a["gate_ps"], 1)

            def ranks(b, n):
                pe.wait_ge(a["total"], b + 1)
                pe.matmul(p_rank[:, 0:G * E], before_b[:],
                          taken[n][:, 0:G, :].rearrange("p j e -> p (j e)"), start=True,
                          stop=False)
                for j in range(G - 1):
                    pe.matmul(p_rank[:, (j + 1) * E:G * E], ones_b[:],
                              taken[n][:, j:j + 1, :].broadcast_to([P, G - 1 - j, E]),
                              start=False, stop=False)
                pe.matmul(p_rank[:, 0:G * E], ones_b[:],
                          taken[n][:, G:G + 1, :].broadcast_to([P, G, E]), start=False,
                          stop=True).then_inc(a["rank_ps"], 1)

            def a_round(i, par):
                now, two, nxt = i, i - 2, i + 1
                steps_of((turn2, two, par), (times_gate, two, par), (times_w_in, now, par),
                         (ranks, two, par), (turn1, nxt, 1 - par), (times_w_out, now, par))

            rounds_of_a(pe, a_round)

            pe.wait_ge(a["place"], B)
            pe.matmul(p_rank[:, 0:E], ones_b[:], taken[B % 2][:, G, :], start=True,
                      stop=True).then_inc(s_count_ps, 1)

            pe.wait_ge(s_table, 1)

            def chunk_of(t):
                return pe.value_load(tile_chunk_i[0:1, bass.ds(t, 1)], min_val=0,
                                     max_val=(E - 1) * FC)

            def layer(to, x_hi, x_lo, first_chunk):
                w_hi, w_lo = (w_parts[:, bass.ds(first_chunk, FC), part, :] for part in (0, 1))
                pe.matmul(to, x_hi, w_hi, start=True, stop=False)
                pe.matmul(to, x_lo, w_hi, start=False, stop=False)
                return pe.matmul(to, x_hi, w_lo, start=False, stop=True)

            chunks = {}

            def c_round(base, r):
                first = 0 if isinstance(base, int) and base == 0 else -LEAD_PE
                t = base + r
                if in_range(t, TILES + 1):
                    wait(pe, c["x_lo"], t)
                if in_range(t, TILES):
                    pe.wait_ge(s_rows_in[r % UNROLL],
                               (16 // UNROLL) * base + 16 * (r // UNROLL + 1))
                    pe.transpose(p_xeT[:, 0:P], taken_rows[r % UNROLL][:, 0:D],
                                 ident[:]).then_inc(c["xeT_ps"], 1)
                t = base + (r - 1)
                if in_range(t, TILES):
                    if isinstance(t, int) and t == 0:
                        pe.wait_ge(s_w_lo[0], 1)
                        pe.wait_ge(s_w_lo[1], 1)
                    if r == first:
                        chunks[r] = chunk_of(t)
                    n = (r - 1) % 2
                    wait(pe, c["silu"], t)
                    layer(p_l1[:], x_hi[n][:], x_lo[n][:], chunks[r]).then_inc(c["l1_ps"], 1)
                    wait(pe, c["gated"], t)
                    layer(p_l2[:], x_hi[n][:], x_lo[n][:],
                          chunks[r] + W_CHUNKS).then_inc(c["l2_ps"], 1)
                if r + 1 < UNROLL_PE - LEAD_PE and in_range(base + r, TILES):
                    chunks[r + 1] = chunk_of(base + r)
                if in_range(base + (r - 3), TILES):
                    chunk = chunks[r - 2] if r >= first + 2 else chunk_of(base + (r - 3))
                t = base + (r - 2)
                if in_range(t, TILES + 1):
                    wait(pe, c["gatedT"], t)
                if in_range(t, TILES):
                    if isinstance(t, int) and t == TILES - 1:
                        pe.wait_ge(c["gated"], TILES)
                    for n in range(FC):
                        last = pe.transpose(p_gatedT[:, n * P:(n + 1) * P],
                                            gated[r % 2][:, n * P:(n + 1) * P], ident[:])
                    last.then_inc(c["gatedT_ps"], 1)
                t = base + (r - 3)
                if in_range(t, TILES):
                    if isinstance(t, int) and t == 0:
                        pe.wait_ge(s_w_in[2], 16)
                    wait(pe, c["y"], t - 1)
                    for n in range(FC):
                        wo = w_raw_chunks[:, bass.ds(chunk + (2 * W_CHUNKS + n), 1), :]
                        last = pe.matmul(p_y[(r - 3) % 2][:, 0:D],
                                         gatedT[(r - 3) % 2][:, n * P:(n + 1) * P],
                                         wo.rearrange("p o d -> p (o d)"), start=(n == 0),
                                         stop=(n == FC - 1))
                    last.then_inc(c["y_ps"], 1)

            rounds_of_tiles(pe, c_round, UNROLL_PE, LEAD_PE)


_INS = ["L0_attn_x", "L0_attn_W_in", "L0_attn_b_in", "L0_attn_W_out", "L0_attn_b_out",
        "L0_attn_decay", "L0_attn_mix", "L0_ffn_gate_kernel", "L0_ffn_w0", "L0_ffn_w1",
        "L0_ffn_wo"]


def kernel(**inputs):
    import numpy as np
    import concourse.bacc as bacc
    from concourse import mybir as _mybir
    from concourse.bass_utils import run_bass_kernel_spmd

    nc = bacc.Bacc("TRN2", target_bir_lowering=False, num_devices=1)
    arrays, args = {}, []
    for name in _INS:
        array = np.ascontiguousarray(inputs[name]).reshape(np.shape(inputs[name]) or (1,))
        arrays["in_" + name] = array
        args.append(nc.dram_tensor("in_" + name, array.shape, _mybir.dt.from_np(array.dtype),
                                   kind="ExternalInput").ap())
    out = nc.dram_tensor("out_dram", (B, S, D), F32, kind="ExternalOutput").ap()
    sandwich_kernel(nc, *args, out)
    r = run_bass_kernel_spmd(nc, [arrays], core_ids=[0])
    return r.results[0]["out_dram"]
```
